# Optimizing a Trainium2 kernel written in Bass

```python
import numpy as np
import jax
import jax.numpy as jnp

def _softmax(x, axis=-1):
    return jax.nn.softmax(x, axis=axis)

def _gelu(x):
    return jax.nn.gelu(x, approximate=True)

def _silu(x):
    return jax.nn.silu(x)

def _sigmoid(x):
    return jax.nn.sigmoid(x)

def _layernorm(x, axis=-1, eps=1e-05):
    m = jnp.mean(x, axis=axis, keepdims=True)
    v = jnp.var(x, axis=axis, keepdims=True)
    return (x - m) / jnp.sqrt(v + eps)

def _scatter_add(tgt, idx, src, axis=0):
    return tgt.at[idx].add(src)

def _segment_sum(src, seg, n):
    return jax.ops.segment_sum(src, seg, n)
kernel_name = 'mk_macaron_d2_jaxref_r8_185e1e'

def setup_inputs(seed: int=0):
    np.random.seed(seed)
    _w = jnp.asarray

    def _L0_attn_setup():
        import jax, jax.numpy as jnp
        import numpy as np
        D_MODEL = 128
        NHEAD = 16
        HEAD_DIM = D_MODEL // NHEAD
        SCALE = float(np.sqrt(HEAD_DIM))
        key = jax.random.key(seed)
        ks = jax.random.split(key, 6)
        B, T = (2, 256)
        x = jax.random.normal(ks[0], (B, T, D_MODEL), dtype=jnp.float32)
        s = 1.0 / np.sqrt(D_MODEL)
        qkv_w = jax.random.uniform(ks[1], (3 * D_MODEL, D_MODEL), jnp.float32, -s, s)
        qkv_b = jax.random.uniform(ks[2], (3 * D_MODEL,), jnp.float32, -s, s)
        out_w = jax.random.uniform(ks[3], (D_MODEL, D_MODEL), jnp.float32, -s, s)
        out_b = jax.random.uniform(ks[4], (D_MODEL,), jnp.float32, -s, s)
        decay_alpha = jnp.full((NHEAD,), 0.1, dtype=jnp.float32)
        return {'x': x, 'qkv_w': qkv_w, 'qkv_b': qkv_b, 'out_w': out_w, 'out_b': out_b, 'decay_alpha': decay_alpha}
    _L0_attn_in = _L0_attn_setup()

    def _L0_ffn_setup():
        import jax, jax.numpy as jnp
        import numpy as np
        NUM_EXPERTS = 160
        TOP_K = 8
        ROUTED_SCALE = 2.5
        HIDDEN = 128
        INTER = 64
        key = jax.random.key(seed)
        ks = jax.random.split(key, 7)
        B, S = (1, 256)
        return {'hidden_states': jax.random.normal(ks[0], (B, S, HIDDEN), dtype=jnp.float32), 'router_w': jax.random.normal(ks[1], (NUM_EXPERTS, HIDDEN), dtype=jnp.float32) * 0.02, 'expert_bias': jnp.zeros((NUM_EXPERTS,), dtype=jnp.float32), 'w_gate': jax.random.normal(ks[2], (NUM_EXPERTS, INTER, HIDDEN), dtype=jnp.float32) * 0.02, 'w_down': jax.random.normal(ks[3], (NUM_EXPERTS, HIDDEN, INTER), dtype=jnp.float32) * 0.02, 'w_gate_shared': jax.random.normal(ks[4], (INTER, HIDDEN), dtype=jnp.float32) * 0.02, 'w_down_shared': jax.random.normal(ks[5], (HIDDEN, INTER), dtype=jnp.float32) * 0.02}
    _L0_ffn_in = _L0_ffn_setup()

    def _L1_attn_setup():
        import jax, jax.numpy as jnp
        import numpy as np
        DIM = 128
        H = 16
        KV = 2
        D = DIM // H
        W = 32
        HW = W // 2
        key = jax.random.key(seed)
        ks = jax.random.split(key, 9)
        B, S = (2, 512)
        n = lambda k, shp, sc=1.0: jax.random.normal(k, shp, jnp.float32) * sc
        return {'x': n(ks[0], (B, S, DIM)), 'Wq': n(ks[1], (DIM, H * D), 0.02), 'bq': n(ks[2], (H * D,), 0.02), 'Wk': n(ks[3], (DIM, KV * D), 0.02), 'bk': n(ks[4], (KV * D,), 0.02), 'Wv': n(ks[5], (DIM, KV * D), 0.02), 'bv': n(ks[6], (KV * D,), 0.02), 'Wo': n(ks[7], (DIM, DIM), 0.02), 'bo': n(ks[8], (DIM,), 0.02)}
    _L1_attn_in = _L1_attn_setup()

    def _L1_ffn_setup():
        import jax, jax.numpy as jnp
        import numpy as np
        LORA_DIM = 16
        LORA_TOKEN_INDEX = 1
        B, S, D, H = (4, 256, 128, 512)
        key = jax.random.key(seed)
        ks = jax.random.split(key, 6)
        x = jax.random.normal(ks[0], (B, S, D), dtype=jnp.float32)
        W1 = jax.random.normal(ks[1], (H, D), dtype=jnp.float32) * 0.02
        b1 = jnp.zeros((H,), dtype=jnp.float32)
        W2 = jax.random.normal(ks[2], (D, H), dtype=jnp.float32) * 0.02
        b2 = jnp.zeros((D,), dtype=jnp.float32)
        scale = jnp.asarray(0.001, dtype=jnp.float32)
        return {'x': x, 'W1': W1, 'b1': b1, 'W2': W2, 'b2': b2, 'scale': scale}
    _L1_ffn_in = _L1_ffn_setup()
    _d = {'L0_attn_x': _L0_attn_in['x'], 'L0_attn_qkv_w': _L0_attn_in['qkv_w'], 'L0_attn_qkv_b': _L0_attn_in['qkv_b'], 'L0_attn_out_w': _L0_attn_in['out_w'], 'L0_attn_out_b': _L0_attn_in['out_b'], 'L0_attn_decay_alpha': _L0_attn_in['decay_alpha'], 'L0_ffn_router_w': _L0_ffn_in['router_w'], 'L0_ffn_expert_bias': _L0_ffn_in['expert_bias'], 'L0_ffn_w_gate': _L0_ffn_in['w_gate'], 'L0_ffn_w_down': _L0_ffn_in['w_down'], 'L0_ffn_w_gate_shared': _L0_ffn_in['w_gate_shared'], 'L0_ffn_w_down_shared': _L0_ffn_in['w_down_shared'], 'L1_attn_Wq': _L1_attn_in['Wq'], 'L1_attn_bq': _L1_attn_in['bq'], 'L1_attn_Wk': _L1_attn_in['Wk'], 'L1_attn_bk': _L1_attn_in['bk'], 'L1_attn_Wv': _L1_attn_in['Wv'], 'L1_attn_bv': _L1_attn_in['bv'], 'L1_attn_Wo': _L1_attn_in['Wo'], 'L1_attn_bo': _L1_attn_in['bo'], 'L1_ffn_W1': _L1_ffn_in['W1'], 'L1_ffn_b1': _L1_ffn_in['b1'], 'L1_ffn_W2': _L1_ffn_in['W2'], 'L1_ffn_b2': _L1_ffn_in['b2'], 'L1_ffn_scale': _L1_ffn_in['scale']}
    _x0 = _d['L0_attn_x']
    _d['L0_attn_x'] = jax.random.normal(jax.random.fold_in(jax.random.key(seed), 1), (16, 256, 128), dtype=_x0.dtype)
    del _x0
    return _d

def reference(L0_attn_x, L0_attn_qkv_w, L0_attn_qkv_b, L0_attn_out_w, L0_attn_out_b, L0_attn_decay_alpha, L0_ffn_router_w, L0_ffn_expert_bias, L0_ffn_w_gate, L0_ffn_w_down, L0_ffn_w_gate_shared, L0_ffn_w_down_shared, L1_attn_Wq, L1_attn_bq, L1_attn_Wk, L1_attn_bk, L1_attn_Wv, L1_attn_bv, L1_attn_Wo, L1_attn_bo, L1_ffn_W1, L1_ffn_b1, L1_ffn_W2, L1_ffn_b2, L1_ffn_scale):

    def _L0_attn_ref(x, qkv_w, qkv_b, out_w, out_b, decay_alpha):
        import jax, jax.numpy as jnp
        import numpy as np
        D_MODEL = 128
        NHEAD = 16
        HEAD_DIM = D_MODEL // NHEAD
        SCALE = float(np.sqrt(HEAD_DIM))
        B, T, D = x.shape
        qkv = x @ qkv_w.T + qkv_b
        qkv = qkv.reshape(B, T, 3, NHEAD, HEAD_DIM).transpose(2, 0, 3, 1, 4)
        q, k, v = (qkv[0], qkv[1], qkv[2])
        logits = jnp.einsum('bhqd,bhkd->bhqk', q, k) / SCALE
        pos = jnp.arange(T, dtype=jnp.float32)
        dist = jnp.abs(pos[None, :] - pos[:, None])
        alpha = jax.nn.softplus(decay_alpha)
        logits = logits - alpha[:, None, None] * dist[None]
        attn = jax.nn.softmax(logits, axis=-1)
        out = jnp.einsum('bhqk,bhkd->bhqd', attn, v)
        out = out.transpose(0, 2, 1, 3).reshape(B, T, D)
        out = out @ out_w.T + out_b
        return out

    def _L0_ffn_ref(hidden_states, router_w, expert_bias, w_gate, w_down, w_gate_shared, w_down_shared):
        import jax, jax.numpy as jnp
        import numpy as np
        NUM_EXPERTS = 160
        TOP_K = 8
        ROUTED_SCALE = 2.5
        HIDDEN = 128
        INTER = 64
        B, S, H = hidden_states.shape
        x = hidden_states.reshape(-1, H)
        T = x.shape[0]
        logits = x @ router_w.T + expert_bias[None, :]
        probs = jax.nn.sigmoid(logits)
        top_w, top_idx = jax.lax.top_k(probs, TOP_K)
        top_w = top_w / (jnp.sum(top_w, axis=-1, keepdims=True) + 1e-09)
        top_w = top_w * ROUTED_SCALE
        combine = jnp.zeros((T, NUM_EXPERTS), dtype=x.dtype)
        combine = combine.at[jnp.arange(T)[:, None], top_idx].set(top_w)
        h1 = jax.nn.silu(jnp.einsum('th,eih->eti', x, w_gate))
        h1w = h1 * combine.T[:, :, None]
        routed = jnp.einsum('eti,ehi->th', h1w, w_down)
        shared = jax.nn.silu(x @ w_gate_shared.T) @ w_down_shared.T
        return (routed + shared).reshape(B, S, H)

    def _L1_attn_ref(x, Wq, bq, Wk, bk, Wv, bv, Wo, bo):
        import jax, jax.numpy as jnp
        import numpy as np
        DIM = 128
        H = 16
        KV = 2
        D = DIM // H
        W = 32
        HW = W // 2
        B, S, _ = x.shape
        q = (x @ Wq + bq).reshape(B, S, H, D).transpose(0, 2, 1, 3)
        k = (x @ Wk + bk).reshape(B, S, KV, D).transpose(0, 2, 1, 3)
        v = (x @ Wv + bv).reshape(B, S, KV, D).transpose(0, 2, 1, 3)
        rep = H // KV
        k = jnp.repeat(k, rep, axis=1)
        v = jnp.repeat(v, rep, axis=1)
        pad = ((0, 0), (0, 0), (HW, HW), (0, 0))
        pk = jnp.pad(k, pad)
        pv = jnp.pad(v, pad)
        nblk = S // W
        pk = pk.reshape(B, H, nblk + 1, W, D)
        pv = pv.reshape(B, H, nblk + 1, W, D)
        kb = jnp.concatenate([pk[:, :, :-1], pk[:, :, 1:]], axis=3)
        vb = jnp.concatenate([pv[:, :, :-1], pv[:, :, 1:]], axis=3)
        qb = q.reshape(B, H, nblk, W, D)
        scores = jnp.einsum('bhntd,bhnud->bhntu', qb, kb)
        t = jnp.arange(W)[:, None]
        u = jnp.arange(2 * W)[None, :]
        win_mask = (u >= t) & (u < t + W)
        scores = jnp.where(win_mask, scores, -jnp.inf)
        probs = jax.nn.softmax(scores, axis=-1)
        out = jnp.einsum('bhntu,bhnud->bhntd', probs, vb)
        out = out.reshape(B, H, S, D).transpose(0, 2, 1, 3).reshape(B, S, H * D)
        return out @ Wo + bo

    def _L1_ffn_ref(x, W1, b1, W2, b2, scale):
        import jax, jax.numpy as jnp
        import numpy as np
        LORA_DIM = 16
        LORA_TOKEN_INDEX = 1
        B, S, D, H = (4, 256, 128, 512)
        Bx, Sx, Dx = x.shape
        Hx = W1.shape[0]
        lt = jax.lax.dynamic_slice_in_dim(x, LORA_TOKEN_INDEX, LORA_DIM, axis=1)
        even = lt[:, ::2, :]
        odd = lt[:, 1::2, :]
        m1 = (even[:, :4, :, None] * odd[:, :4, None, :]).reshape(Bx, Hx, Dx)
        m2 = (even[:, 4:, :, None] * odd[:, 4:, None, :]).reshape(Bx, Dx, Hx)
        h = jnp.einsum('bsd,hd->bsh', x, W1) + scale * jnp.einsum('bsd,bhd->bsh', x, m1) + b1
        h = jax.nn.gelu(h, approximate=False)
        out = jnp.einsum('bsh,oh->bso', h, W2) + scale * jnp.einsum('bsh,boh->bso', h, m2) + b2
        return out
    x = L0_attn_x
    x = x + 0.5 * _L0_ffn_ref(_layernorm(x, axis=-1), L0_ffn_router_w, L0_ffn_expert_bias, L0_ffn_w_gate, L0_ffn_w_down, L0_ffn_w_gate_shared, L0_ffn_w_down_shared)
    x = x + _L0_attn_ref(_layernorm(x, axis=-1), L0_attn_qkv_w, L0_attn_qkv_b, L0_attn_out_w, L0_attn_out_b, L0_attn_decay_alpha)
    x = x + 0.5 * _L0_ffn_ref(_layernorm(x, axis=-1), L0_ffn_router_w, L0_ffn_expert_bias, L0_ffn_w_gate, L0_ffn_w_down, L0_ffn_w_gate_shared, L0_ffn_w_down_shared)
    x = x + 0.5 * _L1_ffn_ref(_layernorm(x, axis=-1), L1_ffn_W1, L1_ffn_b1, L1_ffn_W2, L1_ffn_b2, L1_ffn_scale)
    x = x + _L1_attn_ref(_layernorm(x, axis=-1), L1_attn_Wq, L1_attn_bq, L1_attn_Wk, L1_attn_bk, L1_attn_Wv, L1_attn_bv, L1_attn_Wo, L1_attn_bo)
    x = x + 0.5 * _L1_ffn_ref(_layernorm(x, axis=-1), L1_ffn_W1, L1_ffn_b1, L1_ffn_W2, L1_ffn_b2, L1_ffn_scale)
    return x

_drawn_inputs = setup_inputs


def setup_inputs(seed=0):
    import zlib

    import numpy as np

    out = dict(_drawn_inputs(seed))
    spreads = {'L0_attn_decay_alpha': (0.10000000149011612, 0.6),
     'L0_ffn_expert_bias': (0.0, 0.635),
     'L1_ffn_b1': (0.0, 0.344),
     'L1_ffn_b2': (0.0, 0.1)}
    factors = {'L0_ffn_router_w': 3.841,
     'L0_ffn_w_gate': 3.659,
     'L0_ffn_w_down': 3.647,
     'L0_ffn_w_gate_shared': 3.13,
     'L0_ffn_w_down_shared': 3.077,
     'L1_attn_Wq': 8.0,
     'L1_attn_bq': 8.0,
     'L1_attn_Wk': 8.0,
     'L1_attn_bk': 64.0,
     'L1_attn_Wv': 5.731,
     'L1_attn_bv': 8.0,
     'L1_attn_Wo': 5.072,
     'L1_attn_bo': 2.749}
    for name, (base, spread) in spreads.items():
        noise = np.random.default_rng([zlib.crc32(name.encode()), seed]).standard_normal(out[name].shape)
        drawn = base * np.exp(spread * noise) if base else spread * noise
        out[name] = jnp.asarray(drawn.astype(out[name].dtype))
    for name, factor in factors.items():
        out[name] = (out[name] * factor).astype(out[name].dtype)
    return out
```

```python
from contextlib import ExitStack

import numpy as np
import concourse.bass as bass
from concourse import mybir

F32 = mybir.dt.float32
F16 = mybir.dt.float16
ALU = mybir.AluOpType
ACT = mybir.ActivationFunctionType
AX = mybir.AxisListType

P = 128
BATCHES, SEQ, D = 16, 256, 128
TILES = 4
BLK = TILES * P
BLOCKS = BATCHES * SEQ // BLK
NB = BLK // SEQ
QT = SEQ // P
HEADS, HD = 16, 8
HG = HEADS // 4
EXPERTS, INTER, TOPK = 160, 64, 8
ROUTED_SCALE = 2.5
GROUPS = 3
SLOTS = EXPERTS + 2
EG = SLOTS // GROUPS
PAIRS = EG // 2
CHUNKS = PAIRS * GROUPS
PAD = 16
W1KEYS = P + 2 * PAD
HF, HJ = 512, 4
EPS = 1e-5
NEG = -1e30
STAGES = 6
N_PROJ = (2 * HG, HG + 2)
PROJ = sum(N_PROJ)
UNITS = NB * HEADS
LAG = 4
DVE_STEPS = 57

PARAMS = {}
CONSTS = {}
for table, entries in (
    (PARAMS, (("router", EXPERTS), ("ebias", EXPERTS), ("decay", HEADS), ("qk0", 8 * P), ("qb0", 4), ("kb0", 4),
              ("v0", P), ("vb0", P), ("o0", P), ("ob0", P), ("qk1", 6 * P), ("qb1", 4), ("kb1", 2), ("v1", 16),
              ("vb1", 16), ("o1", P), ("ob1", P), ("w1", HF), ("b1", HJ), ("w2", HF), ("b2", P), ("scale", 1))),
    (CONSTS, (("ident", P), ("negdist", 3 * P), ("band", W1KEYS), ("mq", 1), ("mk", 1), ("validA", TILES),
              ("validB", TILES), ("selE1", 4), ("selO1", 4), ("selE2", 4), ("selO2", 4), ("diag", 4),
              ("pow", TILES)))):
    at_col = 0
    for entry, width in entries:
        table[entry] = (at_col, width)
        at_col += width
    table["_all"] = (0, at_col)


def build(nc, x, params, consts, sel16, wmoe, out):
    x_v = x.rearrange("b s d -> (b s) d").rearrange("(i t p) d -> i p t d", p=P, t=TILES)
    out_v = out.rearrange("b s d -> (b s) d").rearrange("(i t p) d -> i p t d", p=P, t=TILES)

    with ExitStack() as ctx:
        def sb(name, shape, dt=F32):
            return ctx.enter_context(nc.sbuf_tensor(name, shape, dt))

        def sem(name):
            return ctx.enter_context(nc.semaphore(name))

        par = sb("par", [P, PARAMS["_all"][1]])
        con = sb("con", [P, CONSTS["_all"][1]])
        sel = sb("sel", [2 * EG, PAIRS, P], F16)
        ident16 = sb("ident16", [P, P], F16)
        wm = sb("wm", [P, PAIRS, 4 * GROUPS, P], F16)
        work = sb("work", [P, 6, BLK])
        decay_tab = sb("decay_tab", [P, HEADS, 3 * P])
        alpha = sb("alpha", [P, 4, HEADS])
        vbA = sb("vbA", [P, TILES, 16])
        vbB = sb("vbB", [32, TILES, 16])
        qb0s = sb("qb0s", [P, 4])
        b2h = sb("b2h", [P, P])
        xin = sb("xin", [P, TILES, P])
        xs = sb("xs", [P, TILES, P])
        xout = sb("xout", [P, TILES, P])
        xn = sb("xn", [P, TILES, P])
        xT = sb("xT", [P, NB, SEQ + 2 * PAD])
        stats = sb("stats", [P, TILES, 6])
        mv = sb("mv", [P, TILES, 2])
        vare = sb("vare", [P, TILES])
        rstd = sb("rstd", [P, TILES])
        xh = sb("xh", [P, BLK], F16)
        xl = sb("xl", [P, BLK], F16)
        probs = sb("probs", [P, TILES, EXPERTS])
        rep = sb("rep", [P, TILES, EXPERTS])
        m8 = sb("m8", [P, TILES, TOPK])
        wsum = sb("wsum", [P, 3, TILES])
        comb = sb("comb", [P, TILES, SLOTS])
        comb16 = sb("comb16", [P, TILES * GROUPS, 2 * EG], F16)
        combT = sb("combT", [2 * EG, GROUPS, BLK], F16)
        shared = sb("shared", [P, 4, BLK])
        att = shared[:, 0, :].rearrange("p (t d) -> p t d", t=TILES)
        attT = shared[:, 1, :]
        yT = shared[:, 2, :]
        big = sb("big", [P, 4, BLK])
        pf = big[:, 0:2, :]
        pT = big[:, 2:4, :]
        qst = sb("qst", [P, HG, BLK], F16)
        kst0 = sb("kst0", [P, HG, NB, SEQ], F16)
        hh = qst[:, 0:GROUPS, :]
        hl = kst0[:, 0:GROUPS, :, :].rearrange("p g b q -> p g (b q)")
        kst1 = sb("kst1", [P, 2, NB, SEQ + 2 * PAD], F16)
        va0 = sb("va0", [P, TILES, HEADS, HD + 1])
        va1 = sb("va1", [P, TILES, 2, HD + 1])
        vb1 = sb("vb1", [32, TILES, 2, HD + 1])
        nmax = sb("nmax", [P, 4, QT])
        rden = sb("rden", [P, NB, 2 * HEADS])
        odd = sb("odd", [4, NB, 2 * P])
        rank = shared[0:4, :, :].rearrange("p (b m) n -> p b m n", b=NB)
        weff = big[:, :, :].rearrange("p (b m) n -> p b m n", b=NB)
        hid = work[:, 0:4, :].rearrange("p (b r) (c q) -> p b (r c) q", b=NB, c=2)

        bank = [ctx.enter_context(nc.psum_tensor(f"bank{n}", [P, 512], F32)) for n in range(8)]
        b_xT = bank[0]

        def pc(name):
            a, w = PARAMS[name]
            return par[:, a:a + w]

        def cc(name, rows=P):
            a, w = CONSTS[name]
            return con[0:rows, a:a + w]

        ident = cc("ident")
        xT_mid = xT[:, :, PAD:PAD + SEQ]

        def xT_tile(t):
            return xT[:, t // QT, PAD + (t % QT) * P:PAD + (t % QT + 1) * P]

        params_in, consts_in, w_in = sem("params_in"), sem("consts_in"), [sem(f"w_in{r}") for r in range(3)]
        w_hi, w_lo = sem("w_hi"), sem("w_lo")
        setup_pool, setup_dve, setup_act, decay_ready = sem("setup_pool"), sem("setup_dve"), sem("setup_act"), sem("decay_ready")
        x_in, x_taken, out_ready, stored = sem("x_in"), sem("x_taken"), sem("out_ready"), sem("stored")
        dve_step, carried = sem("dve_step"), sem("carried")
        var_ready, rstd_ready = sem("var_ready"), sem("rstd_ready")
        xn_ready, xT_raw, xT_ready = sem("xn_ready"), sem("xT_raw"), sem("xT_ready")
        router_raw, logits_ready, probs_ready = sem("router_raw"), sem("logits_ready"), sem("probs_ready")
        x_split, comb_ready = sem("x_split"), sem("comb_ready")
        combT_raw, combT_ready = sem("combT_raw"), sem("combT_ready")
        gate_raw, spread_raw = sem("gate_raw"), sem("spread_raw")
        silu_done, weighted = sem("silu_done"), sem("weighted")
        h_hi, h_lo, h_used = sem("h_hi"), sem("h_lo"), sem("h_used")
        y_raw, y_copied, y_tok = sem("y_raw"), sem("y_copied"), sem("y_tok")
        proj_raw, proj_copied, stacked = sem("proj_raw"), sem("proj_copied"), sem("stacked")
        v_raw, v_ready = sem("v_raw"), sem("v_ready")
        scores_raw, biased, exp_done = sem("scores_raw"), sem("biased"), sem("exp_done")
        pT_raw, pT_act, pT_dve, pv_done = sem("pT_raw"), sem("pT_act"), sem("pT_dve"), sem("pv_done")
        att_ready, attT_raw, attT_ready, out_raw = sem("att_ready"), sem("attT_raw"), sem("attT_ready"), sem("out_raw")
        picked_raw, rank_ready, outer_raw, weff_ready = sem("picked_raw"), sem("rank_ready"), sem("outer_raw"), sem("weff_ready")
        hid_raw, hid_ready, down_raw = sem("hid_raw"), sem("hid_ready"), sem("down_raw")

        def stage(r):
            return work[:].rearrange("p a b -> p (a b)")[:, r * 1024:r * 1024 + 2 * GROUPS * P]

        def piece(m, r, lo):
            return wm[:, m * 3 + r, lo:4 * GROUPS:2, :]

        def spread_bank(g):
            return bank[(4, 5, 7)[g]]

        def y_done(i, u):
            return h_used, i * (2 * CHUNKS) + (u + 1) * CHUNKS

        block = ctx.enter_context(nc.Block())

        @block.sync
        def _(sp):
            sp.dma_start(par[:], params).then_inc(params_in, 16)
            sp.dma_start(con[:], consts).then_inc(consts_in, 16)
            sp.dma_start(xin[:], x_v[0]).then_inc(x_in, 16)
            for r in range(3):
                sp.dma_start(stage(r), wmoe[r]).then_inc(w_in[r], 16)
            sp.dma_start(sel[:], sel16[0:2 * EG, 0:PAIRS * P].rearrange("p (j m) -> p j m", m=P)).then_inc(consts_in, 16)
            sp.dma_start(ident16[:], sel16[:, PAIRS * P:]).then_inc(consts_in, 16)
            assert PAIRS % 3 == 0
            with sp.Fori(1, PAIRS // 3) as m:
                for r in range(3):
                    sp.wait_ge(w_hi, m * 3 + (r - 2))
                    sp.wait_ge(w_lo, m * 3 + (r - 2))
                    sp.dma_start(stage(r), wmoe[m * 3 + r]).then_inc(w_in[r], 16)
            with sp.Fori(0, BLOCKS - 1) as i:
                sp.wait_ge(x_taken, i + 1)
                sp.dma_start(xin[:], x_v[i + 1]).then_inc(x_in, 16)
                sp.wait_ge(out_ready, i + 1)
                sp.dma_start(out_v[i], xout[:]).then_inc(stored, 16)
            sp.wait_ge(out_ready, BLOCKS)
            sp.dma_start(out_v[BLOCKS - 1], xout[:]).then_inc(stored, 16)
            sp.wait_ge(stored, 16 * (BLOCKS + 1))

        @block.gpsimd
        def _(pool):
            nc.gpsimd.memset(xT[:], 0.0).then_inc(setup_pool, 1)
            nc.gpsimd.memset(kst1[:], 0.0).then_inc(setup_pool, 1)
            nc.gpsimd.memset(va0[:], 1.0).then_inc(setup_pool, 1)
            nc.gpsimd.memset(va1[:], 1.0).then_inc(setup_pool, 1)
            nc.gpsimd.memset(vb1[:], 1.0).then_inc(setup_pool, 1)
            nc.gpsimd.memset(comb[:, :, EXPERTS:EXPERTS + 1], 1.0).then_inc(setup_pool, 1)
            nc.gpsimd.memset(comb[:, :, EXPERTS + 1:], 0.0).then_inc(setup_pool, 1)
            pool.wait_ge(consts_in, 48)
            pool.wait_ge(setup_dve, 5)
            for h in range(HEADS):
                nc.gpsimd.tensor_scalar(decay_tab[:, h, :], cc("negdist"), alpha[:, 3, h:h + 1], None,
                                        ALU.mult).then_inc(decay_ready, 1)
            with pool.Fori(0, BLOCKS) as i:
                for s in range(STAGES):
                    pool.wait_ge(var_ready, i * STAGES + (s + 1))
                    nc.gpsimd.tensor_tensor(rstd[:], vare[:], cc("pow"), ALU.pow).then_inc(rstd_ready, 1)

        @block.tensor
        def _(pe):
            pe.wait_ge(consts_in, 48)
            pe.wait_ge(params_in, 16)
            pe.wait_ge(setup_pool, 7)
            pe.wait_ge(w_hi, PAIRS)
            pe.wait_ge(w_lo, PAIRS)

            with pe.Fori(0, BLOCKS) as i:
                def transposes(s):
                    pe.wait_ge(xn_ready, i * STAGES + (s + 1))
                    for t in range(TILES):
                        mm = nc.tensor.transpose(b_xT[:, t * P:(t + 1) * P], xn[:, t, :], ident)
                    mm.then_inc(xT_raw, 1)
                    pe.wait_ge(xT_ready, i * STAGES + (s + 1))

                def moe(s, u):
                    transposes(s)
                    for t in range(TILES):
                        mm = nc.tensor.matmul(bank[1 + t // 2][:, (t % 2) * 256:(t % 2) * 256 + EXPERTS],
                                              xT_tile(t), pc("router"), start=True, stop=True)
                    mm.then_inc(router_raw, 1)
                    pe.wait_ge(comb_ready, i * 2 + (u + 1))
                    for g in range(GROUPS):
                        dst = bank[4 + g // 2][:, (g % 2) * 256:(g % 2 + 1) * 256].bitcast(F16)
                        for t in range(TILES):
                            mm = nc.tensor.transpose(dst[0:2 * EG, t * P:(t + 1) * P],
                                                     comb16[:, t * GROUPS + g, :], ident16[:, :])
                    mm.then_inc(combT_raw, 1)
                    pe.wait_ge(combT_ready, i * 2 + (u + 1))
                    pe.wait_ge(x_split, i * 2 + (u + 1))
                    n0 = pe.snap(i * (2 * CHUNKS) + u * CHUNKS)

                    def gate(j, g):
                        nc.tensor.matmul(bank[1 + g][:, :], wm[:, j, 4 * g, :], xh[:, :], start=True, stop=False)
                        nc.tensor.matmul(bank[1 + g][:, :], wm[:, j, 4 * g, :], xl[:, :], start=False, stop=False)
                        nc.tensor.matmul(bank[1 + g][:, :], wm[:, j, 4 * g + 1, :], xh[:, :],
                                         start=False, stop=True).then_inc(gate_raw, 1)

                    def spread(j, g):
                        nc.tensor.matmul(spread_bank(g)[:, :], sel[:, j, :], combT[:, g, :],
                                         start=True, stop=True).then_inc(spread_raw, 1)

                    def down(j, g, first, last):
                        nc.tensor.matmul(bank[6][:, :], wm[:, j, 4 * g + 2, :], hh[:, g, :],
                                         start=first, stop=False)
                        nc.tensor.matmul(bank[6][:, :], wm[:, j, 4 * g + 3, :], hh[:, g, :],
                                         start=False, stop=False)
                        nc.tensor.matmul(bank[6][:, :], wm[:, j, 4 * g + 2, :], hl[:, g, :],
                                         start=False, stop=last).then_inc(h_used, 1)

                    for g in range(GROUPS):
                        gate(0, g)
                        spread(0, g)

                    def steady(j, first):
                        n = pe.snap(n0 + j * GROUPS)
                        for g in range(GROUPS):
                            pe.wait_ge(silu_done, n + (g - 2))
                            gate(j, g)
                            pe.wait_ge(weighted, n + (g - 2))
                            spread(j, g)
                            pe.wait_ge(h_lo, n + (g - 2))
                            down(j - 1, g, first and g == 0, False)

                    steady(1, True)
                    with pe.Fori(2, PAIRS) as j:
                        steady(j, False)
                    for g in range(GROUPS):
                        pe.wait_ge(h_lo, n0 + (CHUNKS - GROUPS + g + 1))
                        down(PAIRS - 1, g, False, g == GROUPS - 1)
                    pe.wait_ge(y_copied, i * 2 + (u + 1))
                    for t in range(TILES):
                        mm = nc.tensor.transpose(b_xT[:, t * P:(t + 1) * P], yT[:, t * P:(t + 1) * P], ident)
                    mm.then_inc(y_tok, 1)

                def attention(s, a):
                    transposes(s)
                    wq = pc("qk0" if a == 0 else "qk1")
                    p0 = a * N_PROJ[0]
                    for n in range(N_PROJ[a]):
                        if n >= 3:
                            pe.wait_ge(proj_copied, i * PROJ + (p0 + n - 2))
                        nc.tensor.matmul(bank[1 + n % 3][:, :], wq[:, n * P:(n + 1) * P], xT_mid,
                                         start=True, stop=True).then_inc(proj_raw, 1)
                    for t in range(TILES):
                        if a == 0:
                            mm = nc.tensor.matmul(bank[7][:, t * P:(t + 1) * P], xT_tile(t), pc("v0"),
                                                  start=True, stop=True)
                        else:
                            b, w0 = t // QT, (t % QT) * P
                            nc.tensor.matmul(bank[7][:, t * 16:(t + 1) * 16], xT[:, b, w0:w0 + P], pc("v1"),
                                             start=True, stop=True)
                            mm = nc.tensor.matmul(bank[7][0:32, 64 + t * 16:64 + (t + 1) * 16],
                                                  xT[:, b, w0 + P:w0 + W1KEYS], pc("v1"), start=True, stop=True)
                    mm.then_inc(v_raw, 1)

                    u0 = a * UNITS

                    def scores(n):
                        b, h = n // HEADS, n % HEADS
                        rows = slice(32 * (h % 4), 32 * (h % 4) + 32)
                        if n >= 4:
                            pe.wait_ge(biased, i * (2 * UNITS) + (u0 + n - 3))
                        for qt in range(QT):
                            lhs = qst[rows, h // 4, b * SEQ + qt * P:b * SEQ + (qt + 1) * P]
                            if a == 0:
                                rhs, keys = kst0[rows, h // 4, b, :], SEQ
                            else:
                                rhs, keys = kst1[rows, h // 8, b, qt * P:qt * P + W1KEYS], W1KEYS
                            mm = nc.tensor.matmul(bank[1 + h % 4][:, qt * 256:qt * 256 + keys], lhs, rhs,
                                                  start=True, stop=True)
                        mm.then_inc(scores_raw, 1)

                    def probs_T(n):
                        pe.wait_ge(exp_done, i * (2 * UNITS) + (u0 + n + 1))
                        if n >= 2:
                            wait_pT(n - 2)
                        dst, src = bank[5 + n % 2], work[:, 3 + n % 3, :]
                        for qt in range(QT):
                            nc.tensor.transpose(dst[:, qt * P:(qt + 1) * P], src[:, qt * 256:qt * 256 + P], ident)
                        for qt in range(QT):
                            if a == 0:
                                mm = nc.tensor.transpose(dst[:, (2 + qt) * P:(3 + qt) * P],
                                                         src[:, qt * 256 + P:qt * 256 + 2 * P], ident)
                            else:
                                mm = nc.tensor.transpose(dst[0:32, (2 + qt) * P:(3 + qt) * P],
                                                         src[:, qt * 256 + P:qt * 256 + W1KEYS], ident)
                        mm.then_inc(pT_raw, 1)

                    def wait_pT(n):
                        pe.wait_ge(pT_act if n % 2 == 0 else pT_dve, i * UNITS + (u0 // 2 + n // 2 + 1))

                    def values(n):
                        b, h = n // HEADS, n % HEADS
                        wait_pT(n)
                        o = bank[0 if b == 0 else 7]
                        for qt in range(QT):
                            t = b * QT + qt
                            dst = o[:, (qt * HEADS + h) * 9:(qt * HEADS + h) * 9 + 9]
                            first = pT[:, n % 2, qt * P:(qt + 1) * P]
                            if a == 0:
                                second = pT[:, n % 2, (2 + qt) * P:(3 + qt) * P]
                                nc.tensor.matmul(dst, first, va0[:, b * QT, h, :], start=True, stop=False)
                                mm = nc.tensor.matmul(dst, second, va0[:, b * QT + 1, h, :], start=False, stop=True)
                            else:
                                second = pT[0:32, n % 2, (2 + qt) * P:(3 + qt) * P]
                                nc.tensor.matmul(dst, first, va1[:, t, h // 8, :], start=True, stop=False)
                                mm = nc.tensor.matmul(dst, second, vb1[:, t, h // 8, :], start=False, stop=True)
                        mm.then_inc(pv_done, 1)

                    pe.wait_ge(stacked, i * PROJ + (p0 + N_PROJ[a]))
                    for k in range(UNITS // 4 + 1):
                        if k < UNITS // 4:
                            for hh_ in range(4):
                                scores(4 * k + hh_)
                        if k == 1:
                            pe.wait_ge(v_ready, i * 2 + (a + 1))
                        if k >= 1:
                            for hh_ in range(4):
                                n = 4 * (k - 1) + hh_
                                probs_T(n)
                                if n >= 1:
                                    values(n - 1)
                    values(UNITS - 1)
                    pe.wait_ge(att_ready, i * 2 + (a + 1))
                    for t in range(TILES):
                        mm = nc.tensor.transpose(bank[1][:, t * P:(t + 1) * P], att[:, t, :], ident)
                    mm.then_inc(attT_raw, 1)
                    pe.wait_ge(attT_ready, i * 2 + (a + 1))
                    for t in range(TILES):
                        mm = nc.tensor.matmul(bank[2][:, t * P:(t + 1) * P], attT[:, t * P:(t + 1) * P],
                                              pc("o0" if a == 0 else "o1"), start=True, stop=True)
                    mm.then_inc(out_raw, 1)

                def ffn(s, u):
                    transposes(s)
                    for b in range(NB):
                        if b == 1:
                            pe.wait_ge(rank_ready, i * 4 + (2 * u + b))
                        rows = xn[:, b * QT, :]
                        nc.tensor.matmul(bank[1][0:4, 0:P], cc("selO1"), rows, start=True, stop=True)
                        nc.tensor.matmul(bank[1][0:4, P:2 * P], cc("selO2"), rows, start=True, stop=True)
                        nc.tensor.matmul(bank[2][0:4, :], cc("selE1"),
                                         rows.unsqueeze(1).broadcast_to([P, 4, P]), start=True, stop=True)
                        for r in range(HJ):
                            mm = nc.tensor.matmul(bank[3][0:4, r * P:(r + 1) * P], cc("selE2"),
                                                  rows.rearrange("p (q r) -> p r q", r=4)[:, r, :].unsqueeze(1)
                                                  .broadcast_to([P, 4, 32]), start=True, stop=True)
                        mm.then_inc(picked_raw, 1)
                    for b in range(NB):
                        if b == 1:
                            pe.wait_ge(weff_ready, i * 4 + (2 * u + b))
                        pe.wait_ge(rank_ready, i * 4 + (2 * u + b + 1))
                        for m in range(2):
                            mm = nc.tensor.matmul(bank[4 + m][:, :], odd[:, b, m * P:(m + 1) * P],
                                                  rank[:, b, m, :], start=True, stop=True)
                        mm.then_inc(outer_raw, 1)
                    for b in range(NB):
                        pe.wait_ge(weff_ready, i * 4 + (2 * u + b + 1))
                        for half in range(2):
                            if b == 1:
                                pe.wait_ge(hid_ready, i * 8 + (4 * u + half + 1))
                            for jj in range(2):
                                j = 2 * half + jj
                                mm = nc.tensor.matmul(bank[6 + half][:, jj * SEQ:(jj + 1) * SEQ],
                                                      weff[:, b, 0, j * P:(j + 1) * P], xT_mid[:, b, :],
                                                      start=True, stop=True)
                            mm.then_inc(hid_raw, 1)
                    for b in range(NB):
                        pe.wait_ge(hid_ready, i * 8 + (4 * u + 2 * b + 2))
                        for tt in range(QT):
                            t = b * QT + tt
                            for r in range(HJ):
                                mm = nc.tensor.matmul(b_xT[:, t * P:(t + 1) * P],
                                                      hid[:, b, r, tt * P:(tt + 1) * P],
                                                      weff[:, b, 1, r * P:(r + 1) * P],
                                                      start=(r == 0), stop=(r == HJ - 1))
                    mm.then_inc(down_raw, 1)

                moe(0, 0)
                attention(1, 0)
                moe(2, 1)
                ffn(3, 0)
                attention(4, 1)
                ffn(5, 1)

        @block.scalar
        def _(act):
            act.wait_ge(setup_dve, 1)
            nc.scalar.activation(alpha[:, 1, :], alpha[:, 0, :], ACT.Exp, scale=-1.0).then_inc(setup_act, 1)
            act.wait_ge(setup_act, 1)
            nc.scalar.activation(alpha[:, 2, :], alpha[:, 1, :], ACT.Ln, bias=1.0).then_inc(setup_act, 1)
            with act.Fori(0, PAIRS // 3) as m:
                for r in range(3):
                    act.wait_ge(w_in[r], m * 16 + 16)
                    nc.scalar.copy(piece(m, r, 0), stage(r).rearrange("p (c n) -> p c n", n=P)).then_inc(w_hi, 1)

            with act.Fori(0, BLOCKS) as i:
                def copy_xT(s):
                    act.wait_ge(xT_raw, i * STAGES + (s + 1))
                    nc.scalar.copy(xT_mid, b_xT[:, :].rearrange("p (b q) -> p b q", b=NB)).then_inc(xT_ready, 1)

                def moe(s, u):
                    copy_xT(s)
                    act.wait_ge(logits_ready, i * 2 + (u + 1))
                    nc.scalar.activation(probs[:], rep[:], ACT.Sigmoid).then_inc(probs_ready, 1)
                    act.wait_ge(combT_raw, i * 2 + (u + 1))
                    nc.scalar.copy(combT[:, 0:2, :], bank[4][0:2 * EG, :].bitcast(F16)
                                   .rearrange("p (g n) -> p g n", g=2))
                    nc.scalar.copy(combT[:, 2, :], bank[5][0:2 * EG, 0:256].bitcast(F16)).then_inc(combT_ready, 1)
                    n0 = act.snap(i * (2 * CHUNKS) + u * CHUNKS)

                    def silu(n, g, first):
                        act.wait_ge(gate_raw, n + (g + 1))
                        if not first:
                            act.wait_ge(weighted, n + (g - 2))
                        nc.scalar.activation(work[:, g, :], bank[1 + g][:, :], ACT.Silu).then_inc(silu_done, 1)

                    def high(n, g, first):
                        act.wait_ge(weighted, n + (g + 1))
                        if not first:
                            act.wait_ge(h_used, n + (g - 2))
                        nc.scalar.copy(hh[:, g, :], work[:, 3 + g, :]).then_inc(h_hi, 1)

                    silu(n0, 0, True)
                    silu(n0, 1, True)
                    high(n0, 0, True)
                    silu(n0, 2, True)
                    high(n0, 1, True)

                    def steady(j, first):
                        n = act.snap(n0 + j * GROUPS)
                        silu(n, 0, False)
                        high(n + (-GROUPS), 2, first)
                        silu(n, 1, False)
                        high(n, 0, False)
                        silu(n, 2, False)
                        high(n, 1, False)

                    steady(1, True)
                    with act.Fori(2, PAIRS) as j:
                        steady(j, False)
                    high(n0 + (CHUNKS - GROUPS), 2, False)
                    act.wait_ge(y_done(i, u)[0], y_done(i, u)[1])
                    nc.scalar.copy(yT[:, :], bank[6][:, :]).then_inc(y_copied, 1)

                def attention(s, a):
                    copy_xT(s)
                    p0, u0 = a * N_PROJ[0], a * UNITS
                    for n in range(N_PROJ[a]):
                        act.wait_ge(proj_raw, i * PROJ + (p0 + n + 1))
                        if n >= 2:
                            act.wait_ge(stacked, i * PROJ + (p0 + n - 1))
                        if n < HG:
                            bias = qb0s[:, n:n + 1] if a == 0 else pc("qb1")[:, n:n + 1]
                            scale = HD ** -0.5 if a == 0 else 1.0
                        else:
                            bias, scale = pc("kb0" if a == 0 else "kb1")[:, n - HG:n - HG + 1], 1.0
                        nc.scalar.activation(pf[:, n % 2, :], bank[1 + n % 3][:, :], ACT.Identity,
                                             bias=bias, scale=scale).then_inc(proj_copied, 1)
                    keys = SEQ if a == 0 else W1KEYS

                    def exponent(n):
                        act.wait_ge(biased, i * (2 * UNITS) + (u0 + n + 1))
                        if n >= 3:
                            act.wait_ge(pT_raw, i * (2 * UNITS) + (u0 + n - 2))
                        for qt in range(QT):
                            ins = nc.scalar.activation(work[:, 3 + n % 3, qt * 256:qt * 256 + keys],
                                                       work[:, n % 3, qt * 256:qt * 256 + keys], ACT.Exp,
                                                       bias=nmax[:, n % 4, qt:qt + 1], scale=-1.0)
                        ins.then_inc(exp_done, 1)

                    def copy_pT(n):
                        act.wait_ge(pT_raw, i * (2 * UNITS) + (u0 + n + 1))
                        if a == 0:
                            nc.scalar.copy(pT[:, 0, :], bank[5][:, :]).then_inc(pT_act, 1)
                        else:
                            nc.scalar.copy(pT[:, 0, 0:2 * P], bank[5][:, 0:2 * P])
                            nc.scalar.copy(pT[0:32, 0, 2 * P:], bank[5][0:32, 2 * P:]).then_inc(pT_act, 1)

                    for n in range(UNITS + LAG):
                        if n < UNITS:
                            exponent(n)
                        if n >= LAG and n % 2 == 0:
                            copy_pT(n - LAG)
                    act.wait_ge(attT_raw, i * 2 + (a + 1))
                    nc.scalar.copy(attT[:, :], bank[1][:, :]).then_inc(attT_ready, 1)

                def ffn(s, u):
                    copy_xT(s)
                    for b in range(NB):
                        for half in range(2):
                            act.wait_ge(hid_raw, i * 8 + (4 * u + 2 * b + half + 1))
                            for jj in range(2):
                                j = 2 * half + jj
                                ins = nc.scalar.activation(hid[:, b, j, :], bank[6 + half][:, jj * SEQ:(jj + 1) * SEQ],
                                                           ACT.Gelu, bias=pc("b1")[:, j:j + 1])
                            ins.then_inc(hid_ready, 1)

                moe(0, 0)
                attention(1, 0)
                moe(2, 1)
                ffn(3, 0)
                attention(4, 1)
                ffn(5, 1)

        @block.vector
        def _(dve):
            dve.wait_ge(params_in, 16)
            dve.wait_ge(consts_in, 48)
            nc.vector.scalar_tensor_tensor(out=alpha[:, 0, :], in0=pc("decay"), scalar=-1.0, in1=pc("decay"),
                                           op0=ALU.mult, op1=ALU.max).then_inc(setup_dve, 1)
            nc.vector.tensor_scalar(qb0s[:], pc("qb0"), HD ** -0.5, None, ALU.mult).then_inc(setup_dve, 1)
            nc.vector.tensor_scalar(b2h[:], pc("b2"), 0.5, None, ALU.mult).then_inc(setup_dve, 1)
            nc.vector.tensor_tensor(vbA[:], pc("vb1").unsqueeze(1).broadcast_to([P, TILES, 16]),
                                    cc("validA").unsqueeze(2).broadcast_to([P, TILES, 16]), ALU.mult)
            nc.vector.tensor_tensor(vbB[:], pc("vb1")[0:32].unsqueeze(1).broadcast_to([32, TILES, 16]),
                                    cc("validB", 32).unsqueeze(2).broadcast_to([32, TILES, 16]),
                                    ALU.mult).then_inc(setup_dve, 1)
            dve.wait_ge(setup_act, 2)
            nc.vector.scalar_tensor_tensor(out=alpha[:, 3, :], in0=pc("decay"), scalar=0.0, in1=alpha[:, 2, :],
                                           op0=ALU.max, op1=ALU.add).then_inc(setup_dve, 1)
            with dve.Fori(0, PAIRS // 3) as m:
                for r in range(3):
                    dve.wait_ge(w_in[r], m * 16 + 16)
                    dve.wait_ge(w_hi, m * 3 + (r + 1))
                    nc.vector.tensor_tensor(piece(m, r, 1), stage(r).rearrange("p (c n) -> p c n", n=P),
                                            piece(m, r, 0), ALU.subtract).then_inc(w_lo, 1)
            nc.vector.memset(xout[:], 0.0).then_inc(stored, 16)
            dve.wait_ge(stored, 16)
            dve.wait_ge(setup_pool, 7)
            dve.wait_ge(setup_dve, 5)
            dve.wait_ge(decay_ready, HEADS)

            with dve.Fori(0, BLOCKS) as i:
                steps = [0]

                def settle(ins, plain=False):
                    steps[0] += 1
                    ins.then_inc(dve_step, 1)
                    dve.wait_ge(dve_step, i * DVE_STEPS + steps[0])
                    if plain:
                        plain_wait()

                def plain_wait():
                    dve.sem_inc(carried, 1)

                def layer_norm(s):
                    for t in range(TILES):
                        ins = nc.vector.bn_stats(stats[:, t, :], xs[:, t, :])
                    settle(ins, plain=True)
                    for t in range(TILES):
                        ins = nc.vector.bn_aggr(mv[:, t, :], stats[:, t, :])
                    settle(ins)
                    nc.vector.tensor_scalar(vare[:], mv[:, :, 1], EPS, None, ALU.add).then_inc(var_ready, 1)
                    dve.wait_ge(rstd_ready, i * STAGES + (s + 1))
                    for t in range(TILES):
                        ins = nc.vector.tensor_scalar(xn[:, t, :], xs[:, t, :], mv[:, t, 0:1], rstd[:, t:t + 1],
                                                      ALU.subtract, ALU.mult)
                    ins.then_inc(xn_ready, 1)

                def moe(s, u):
                    layer_norm(s)
                    dve.wait_ge(xT_ready, i * STAGES + (s + 1))
                    xh_v = xh[:, :].rearrange("p (b q) -> p b q", b=NB)
                    settle(nc.vector.tensor_copy(xh_v, xT_mid))
                    nc.vector.tensor_tensor(xl[:, :].rearrange("p (b q) -> p b q", b=NB), xT_mid, xh_v,
                                            ALU.subtract).then_inc(x_split, 1)
                    dve.wait_ge(router_raw, i * 2 + (u + 1))
                    for k in range(2):
                        ins = nc.vector.tensor_tensor(
                            rep[:, 2 * k:2 * k + 2, :],
                            bank[1 + k][:, :].rearrange("p (t e) -> p t e", t=2)[:, :, 0:EXPERTS],
                            pc("ebias").unsqueeze(1).broadcast_to([P, 2, EXPERTS]), ALU.add)
                    ins.then_inc(logits_ready, 1)
                    dve.wait_ge(probs_ready, i * 2 + (u + 1))
                    plain_wait()
                    for t in range(TILES):
                        ins = nc.vector.max(m8[:, t, :], probs[:, t, :])
                    settle(ins, plain=True)
                    for t in range(TILES):
                        ins = nc.vector.match_replace(rep[:, t, :], m8[:, t, :], probs[:, t, :], -1.0)
                    settle(nc.vector.tensor_reduce(wsum[:, 0, :], m8[:], AX.X, ALU.add))
                    settle(nc.vector.tensor_scalar(wsum[:, 1, :], wsum[:, 0, :], 1e-9, None, ALU.add))
                    settle(nc.vector.reciprocal(wsum[:, 2, :], wsum[:, 1, :]))
                    settle(nc.vector.tensor_scalar(wsum[:, 0, :], wsum[:, 2, :], ROUTED_SCALE, None, ALU.mult))
                    settle(nc.vector.scalar_tensor_tensor(out=rep[:], in0=rep[:], scalar=0.0, in1=probs[:],
                                                          op0=ALU.is_lt, op1=ALU.mult))
                    settle(nc.vector.tensor_tensor(comb[:, :, 0:EXPERTS], rep[:],
                                                   wsum[:, 0, :].unsqueeze(2).broadcast_to([P, TILES, EXPERTS]),
                                                   ALU.mult))
                    comb_v = comb[:].rearrange("p t (g e) -> p (t g) e", g=GROUPS)
                    settle(nc.vector.tensor_copy(comb16[:, :, 0:EG], comb_v))
                    nc.vector.tensor_tensor(comb16[:, :, EG:], comb_v, comb16[:, :, 0:EG],
                                            ALU.subtract).then_inc(comb_ready, 1)
                    n0 = dve.snap(i * (2 * CHUNKS) + u * CHUNKS)

                    def weigh(n, g, first=False):
                        if not first:
                            dve.wait_ge(h_lo, n + (g - 2))
                        dve.wait_ge(silu_done, n + (g + 1))
                        dve.wait_ge(spread_raw, n + (g + 1))
                        nc.vector.tensor_tensor(work[:, 3 + g, :], work[:, g, :], spread_bank(g)[:, :],
                                                ALU.mult).then_inc(weighted, 1)

                    def low(n, g):
                        dve.wait_ge(h_hi, n + (g + 1))
                        nc.vector.tensor_tensor(hl[:, g, :], work[:, 3 + g, :], hh[:, g, :],
                                                ALU.subtract).then_inc(h_lo, 1)

                    weigh(n0, 0, True)
                    weigh(n0, 1, True)
                    low(n0, 0)
                    weigh(n0, 2, True)
                    low(n0, 1)
                    with dve.Fori(1, PAIRS) as j:
                        n = dve.snap(n0 + j * GROUPS)
                        weigh(n, 0)
                        low(n + (-GROUPS), 2)
                        weigh(n, 1)
                        low(n, 0)
                        weigh(n, 2)
                        low(n, 1)
                    low(n0 + (CHUNKS - GROUPS), 2)
                    dve.wait_ge(y_tok, i * 2 + (u + 1))
                    settle(nc.vector.scalar_tensor_tensor(out=xs[:], in0=tiles_of(b_xT), scalar=0.5, in1=xs[:],
                                                          op0=ALU.mult, op1=ALU.add))

                def attention(s, a):
                    layer_norm(s)
                    p0, u0 = a * N_PROJ[0], a * UNITS
                    for n in range(N_PROJ[a]):
                        phi = (xh, xl)[n % 2]
                        if n >= 2:
                            dve.wait_ge(stacked, i * PROJ + (p0 + n - 1))
                        dve.wait_ge(proj_copied, i * PROJ + (p0 + n + 1))
                        settle(nc.vector.tensor_copy(phi[:, :], pf[:, n % 2, :]))
                        if n < HG:
                            dst, mask = qst[:, n, :].rearrange("p (b q) -> p b q", b=NB), cc("mq")
                        elif a == 0:
                            dst, mask = kst0[:, n - HG, :, :], cc("mk")
                        else:
                            dst, mask = kst1[:, n - HG, :, PAD:PAD + SEQ], cc("mk")
                        nc.vector.scalar_tensor_tensor(
                            out=dst, in0=phi[:, :].rearrange("p (b q) -> p b q", b=NB), scalar=mask,
                            in1=pf[:, n % 2, :].rearrange("p (b q) -> p b q", b=NB),
                            op0=ALU.mult, op1=ALU.add).then_inc(stacked, 1)
                    dve.wait_ge(v_raw, i * 2 + (a + 1))
                    if a == 0:
                        for t in range(TILES):
                            ins = nc.vector.tensor_tensor(
                                va0[:, t, :, 0:HD], bank[7][:, t * P:(t + 1) * P].rearrange("p (h d) -> p h d", d=HD),
                                pc("vb0").rearrange("p (h d) -> p h d", d=HD), ALU.add)
                    else:
                        nc.vector.tensor_tensor(
                            va1[:].rearrange("p t k e -> p (t k) e")[:, :, 0:HD],
                            bank[7][:, 0:64].rearrange("p (c d) -> p c d", d=HD),
                            vbA[:].rearrange("p t (k d) -> p (t k) d", d=HD), ALU.add)
                        ins = nc.vector.tensor_tensor(
                            vb1[:].rearrange("p t k e -> p (t k) e")[:, :, 0:HD],
                            bank[7][0:32, 64:128].rearrange("p (c d) -> p c d", d=HD),
                            vbB[:].rearrange("p t (k d) -> p (t k) d", d=HD), ALU.add)
                    ins.then_inc(v_ready, 1)

                    def bias_scores(n):
                        h = n % HEADS
                        dve.wait_ge(scores_raw, i * (2 * UNITS) + (u0 + n + 1))
                        if n >= 3:
                            dve.wait_ge(exp_done, i * (2 * UNITS) + (u0 + n - 2))
                        plain_wait()
                        for qt in range(QT):
                            if a == 0:
                                keys, table = SEQ, decay_tab[:, h, (1 - qt) * P:(3 - qt) * P]
                            else:
                                keys, table = W1KEYS, cc("band")
                            ins = nc.vector.tensor_tensor_reduce(
                                out=work[:, n % 3, qt * 256:qt * 256 + keys],
                                in0=bank[1 + h % 4][:, qt * 256:qt * 256 + keys], in1=table,
                                scale=-1.0, scalar=3e38, op0=ALU.add, op1=ALU.min,
                                accum_out=nmax[:, n % 4, qt:qt + 1])
                        ins.then_inc(biased, 1)

                    def copy_pT(n):
                        dve.wait_ge(pT_raw, i * (2 * UNITS) + (u0 + n + 1))
                        if a == 0:
                            nc.vector.tensor_copy(pT[:, 1, :], bank[6][:, :]).then_inc(pT_dve, 1)
                        else:
                            nc.vector.tensor_copy(pT[:, 1, 0:2 * P], bank[6][:, 0:2 * P])
                            nc.vector.tensor_copy(pT[0:32, 1, 2 * P:], bank[6][0:32, 2 * P:]).then_inc(pT_dve, 1)

                    for n in range(UNITS + LAG):
                        if n < UNITS:
                            bias_scores(n)
                        if n >= LAG and n % 2 == 1:
                            copy_pT(n - LAG)
                    for b in range(NB):
                        dve.wait_ge(pv_done, i * (2 * UNITS) + (u0 + (b + 1) * HEADS))
                        o = bank[0 if b == 0 else 7][:, 0:2 * HEADS * 9].rearrange("p (c e) -> p c e", e=9)
                        settle(nc.vector.reciprocal(rden[:, b, :], o[:, :, HD]))
                        ins = nc.vector.tensor_tensor(
                            att[:, b * QT:(b + 1) * QT, :].rearrange("p t (h d) -> p (t h) d", d=HD),
                            o[:, :, 0:HD], rden[:, b, :].unsqueeze(2).broadcast_to([P, 2 * HEADS, HD]), ALU.mult)
                    ins.then_inc(att_ready, 1)
                    dve.wait_ge(out_raw, i * 2 + (a + 1))
                    settle(nc.vector.tensor_tensor(xs[:], tiles_of(bank[2]), xs[:], ALU.add))
                    settle(nc.vector.tensor_tensor(xs[:], xs[:], pc("ob0" if a == 0 else "ob1").unsqueeze(1)
                                                   .broadcast_to([P, TILES, P]), ALU.add))

                def ffn(s, u):
                    layer_norm(s)
                    for b in range(NB):
                        dve.wait_ge(picked_raw, i * 4 + (2 * u + b + 1))
                        nc.vector.tensor_copy(odd[:, b, :], bank[1][0:4, 0:2 * P])
                        nc.vector.tensor_tensor(rank[:, b, 0, :].rearrange("p (j q) -> p j q", j=4),
                                                bank[2][0:4, :].rearrange("p (j q) -> p j q", j=4),
                                                cc("diag", 4).unsqueeze(2).broadcast_to([4, 4, P]), ALU.mult)
                        diag2 = cc("diag", 4).unsqueeze(2).broadcast_to([4, 4, 32])
                        for r in range(HJ):
                            ins = nc.vector.tensor_tensor(
                                rank[:, b, 1, r * P:(r + 1) * P].rearrange("p (j q) -> p j q", j=4),
                                bank[3][0:4, r * P:(r + 1) * P].rearrange("p (j q) -> p j q", j=4), diag2, ALU.mult)
                        ins.then_inc(rank_ready, 1)
                    for b in range(NB):
                        dve.wait_ge(outer_raw, i * 4 + (2 * u + b + 1))
                        for m, w in enumerate(("w1", "w2")):
                            ins = nc.vector.scalar_tensor_tensor(out=weff[:, b, m, :], in0=bank[4 + m][:, :],
                                                                 scalar=pc("scale"), in1=pc(w),
                                                                 op0=ALU.mult, op1=ALU.add)
                        ins.then_inc(weff_ready, 1)
                    dve.wait_ge(down_raw, i * 2 + (u + 1))
                    settle(nc.vector.scalar_tensor_tensor(out=xs[:], in0=tiles_of(b_xT), scalar=0.5, in1=xs[:],
                                                          op0=ALU.mult, op1=ALU.add))
                    b2_v = b2h[:].unsqueeze(1).broadcast_to([P, TILES, P])
                    if u == 0:
                        settle(nc.vector.tensor_tensor(xs[:], xs[:], b2_v, ALU.add))
                    else:
                        dve.wait_ge(stored, i * 16 + 16)
                        nc.vector.tensor_tensor(xout[:], xs[:], b2_v, ALU.add).then_inc(out_ready, 1)
                        dve.wait_ge(out_ready, i + 1)

                dve.wait_ge(x_in, i * 16 + 16)
                nc.vector.tensor_copy(xs[:], xin[:]).then_inc(x_taken, 1)
                dve.wait_ge(x_taken, i + 1)
                moe(0, 0)
                attention(1, 0)
                moe(2, 1)
                ffn(3, 0)
                attention(4, 1)
                ffn(5, 1)
                assert steps[0] == DVE_STEPS, steps[0]


def tiles_of(b):
    return b[:, :].rearrange("p (t d) -> p t d", t=TILES)


def lay_out(a):
    f = np.float32

    def rows(v):
        v = np.asarray(v, f).reshape(-1)
        return np.broadcast_to(v, (P, v.size))

    heads = np.array([[(4 * g + hh) * HD + d for hh in range(4) for c in range(4) for d in range(HD)]
                      for g in range(HG)])
    kv = np.array([[k * HD + d for hh in range(4) for c in range(4) for d in range(HD)] for k in range(2)])

    def stacks(w_cols, index):
        return np.concatenate([w_cols[:, ix] for ix in index], axis=1)

    qkv_wT, qkv_b = np.asarray(a["L0_attn_qkv_w"]).T, np.asarray(a["L0_attn_qkv_b"])
    values = {
        "router": np.asarray(a["L0_ffn_router_w"]).T, "ebias": rows(a["L0_ffn_expert_bias"]),
        "decay": rows(a["L0_attn_decay_alpha"]),
        "qk0": np.concatenate([stacks(qkv_wT[:, 0:D], heads), stacks(qkv_wT[:, D:2 * D], heads)], axis=1),
        "qb0": qkv_b[0:D][heads].T, "kb0": qkv_b[D:2 * D][heads].T,
        "v0": qkv_wT[:, 2 * D:], "vb0": rows(qkv_b[2 * D:]),
        "o0": np.asarray(a["L0_attn_out_w"]).T, "ob0": rows(a["L0_attn_out_b"]),
        "qk1": np.concatenate([stacks(np.asarray(a["L1_attn_Wq"]), heads), stacks(np.asarray(a["L1_attn_Wk"]), kv)], axis=1),
        "qb1": np.asarray(a["L1_attn_bq"])[heads].T, "kb1": np.asarray(a["L1_attn_bk"])[kv].T,
        "v1": np.asarray(a["L1_attn_Wv"]), "vb1": rows(a["L1_attn_bv"]),
        "o1": np.asarray(a["L1_attn_Wo"]), "ob1": rows(a["L1_attn_bo"]),
        "w1": np.asarray(a["L1_ffn_W1"]).T, "b1": np.asarray(a["L1_ffn_b1"]).reshape(HJ, P).T,
        "w2": np.asarray(a["L1_ffn_W2"]).T.reshape(HJ, P, D).transpose(1, 0, 2).reshape(P, HJ * D),
        "b2": rows(a["L1_ffn_b2"]), "scale": rows(a["L1_ffn_scale"]),
    }
    params = np.zeros((P, PARAMS["_all"][1]), f)
    for name, v in values.items():
        at, w = PARAMS[name]
        assert v.shape == (P, w), (name, v.shape)
        params[:, at:at + w] = v

    gate = np.concatenate([np.asarray(a["L0_ffn_w_gate"]), np.asarray(a["L0_ffn_w_gate_shared"])[None],
                           np.zeros((1, INTER, D), f)])
    down = np.concatenate([np.asarray(a["L0_ffn_w_down"]), np.asarray(a["L0_ffn_w_down_shared"])[None],
                           np.zeros((1, D, INTER), f)])
    gate = gate.reshape(GROUPS, PAIRS, P, D).transpose(1, 3, 0, 2)
    down = down.transpose(0, 2, 1).reshape(GROUPS, PAIRS, P, D).transpose(1, 2, 0, 3)
    wmoe = np.ascontiguousarray(np.stack([gate, down], axis=3)).reshape(PAIRS, P, 2 * GROUPS * P)
    return params, wmoe


def shape_constants():
    f = np.float32
    p = np.arange(P)
    values = {
        "ident": np.eye(P, dtype=f),
        "negdist": -np.abs(np.arange(3 * P)[None] - P - p[:, None]).astype(f),
        "band": np.where((np.arange(W1KEYS)[None] >= p[:, None]) & (np.arange(W1KEYS)[None] < p[:, None] + 2 * PAD),
                         0.0, NEG).astype(f),
        "mq": np.where(p % 32 >= 16, -1.0, 0.0).astype(f)[:, None],
        "mk": np.where(p % 16 >= 8, -1.0, 0.0).astype(f)[:, None],
        "validA": np.stack([(p >= PAD) | (t % QT > 0) for t in range(TILES)], 1).astype(f),
        "validB": np.stack([(p < PAD) | (t % QT < QT - 1) for t in range(TILES)], 1).astype(f),
        "pow": np.full((P, TILES), -0.5, f),
        "diag": (p[:, None] == np.arange(4)[None]).astype(f),
    }
    for name, first in (("selE1", 1), ("selO1", 2), ("selE2", 9), ("selO2", 10)):
        values[name] = (p[:, None] == first + 2 * np.arange(4)[None]).astype(f)
    consts = np.zeros((P, CONSTS["_all"][1]), f)
    for name, v in values.items():
        at, w = CONSTS[name]
        assert v.shape == (P, w), (name, v.shape)
        consts[:, at:at + w] = v
    sel16 = np.zeros((P, PAIRS * P + P), np.float16)
    for j in range(PAIRS):
        for m in range(P):
            sel16[2 * j + m // INTER, j * P + m] = 1
            sel16[EG + 2 * j + m // INTER, j * P + m] = 1
    sel16[:, PAIRS * P:] = np.eye(P)
    return consts, sel16


def kernel(**inputs):
    import numpy as _np
    import concourse.bacc as _bacc
    from concourse import mybir as _mybir
    from concourse.bass_utils import run_bass_kernel_spmd as _run

    params, wmoe = lay_out(inputs)
    consts, sel16 = shape_constants()
    nc = _bacc.Bacc("TRN2", target_bir_lowering=False, num_devices=1)
    arrays = {"x": _np.ascontiguousarray(inputs["L0_attn_x"]), "params": params, "consts": consts,
              "sel16": sel16, "wmoe": wmoe}
    args = [nc.dram_tensor(name, v.shape, _mybir.dt.from_np(v.dtype), kind="ExternalInput").ap()
            for name, v in arrays.items()]
    out = nc.dram_tensor("out", (BATCHES, SEQ, D), _mybir.dt.float32, kind="ExternalOutput").ap()
    build(nc, *args, out)
    r = _run(nc, [arrays], core_ids=[0])
    return r.results[0]["out"]
```

```python
from contextlib import ExitStack

import numpy as np
import concourse.bass as bass
from concourse import mybir

F32 = mybir.dt.float32
F16 = mybir.dt.float16
ALU = mybir.AluOpType
ACT = mybir.ActivationFunctionType
AX = mybir.AxisListType

P = 128
BATCHES, SEQ, D = 16, 256, 128
TILES = 4
BLK = TILES * P
BLOCKS = BATCHES * SEQ // BLK
NB = BLK // SEQ
QT = SEQ // P
HEADS, HD = 16, 8
HG = HEADS // 4
EXPERTS, INTER, TOPK = 160, 64, 8
ROUTED_SCALE = 2.5
GROUPS = 3
SLOTS = EXPERTS + 2
EG = SLOTS // GROUPS
PAIRS = EG // 2
CHUNKS = PAIRS * GROUPS
PAD = 16
W1KEYS = P + 2 * PAD
HF, HJ = 512, 4
EPS = 1e-5
NEG = -1e30
STAGES = 6
N_PROJ = (2 * HG, HG + 2)
PROJ = sum(N_PROJ)
UNITS = NB * HEADS
GRP = 4
NGRP = UNITS // GRP
HDP = 32
SEGS = (((P, 0, SEQ), (0, 0, SEQ)),
        ((0, 0, P), (P, P - 2 * PAD, P + 2 * PAD), (SEQ + 2 * PAD - P, SEQ - 2 * PAD, 2 * PAD)))
COLS = tuple(sum(n for _, _, n in segs) for segs in SEGS)
LK, LV, LC, LB, LN = 5, 7, 11, 12, 13
SLOTS_A = LN + (NGRP - 1) * GRP + 1
DVE_STEPS = 69

PARAMS = {}
CONSTS = {}
for table, entries in (
    (PARAMS, (("router", EXPERTS), ("ebias", EXPERTS), ("decay", HEADS), ("qk0", 8 * P), ("qb0", 4), ("kb0", 4),
              ("v0", P), ("vb0", P), ("o0", P), ("ob0", P), ("qk1", 6 * P), ("qb1", 4), ("kb1", 2), ("v1", 16),
              ("vb1", 16), ("o1", P), ("ob1", P), ("w1", HF), ("b1", HJ), ("w2", HF), ("b2", P), ("scale", 1))),
    (CONSTS, (("ident", P), ("negdist", 3 * P), ("band", W1KEYS), ("bandT", COLS[1]), ("mq", 1), ("mk", 1), ("valid", 3),
              ("half", 2), ("selE1", 4), ("selO1", 4), ("selE2", 4), ("selO2", 4), ("diag", 4),
              ("pow", TILES)))):
    at_col = 0
    for entry, width in entries:
        table[entry] = (at_col, width)
        at_col += width
    table["_all"] = (0, at_col)


def build(nc, x, params, consts, sel16, wmoe, out):
    x_v = x.rearrange("b s d -> (b s) d").rearrange("(i t p) d -> i p t d", p=P, t=TILES)
    out_v = out.rearrange("b s d -> (b s) d").rearrange("(i t p) d -> i p t d", p=P, t=TILES)

    with ExitStack() as ctx:
        def sb(name, shape, dt=F32):
            return ctx.enter_context(nc.sbuf_tensor(name, shape, dt))

        def sem(name):
            return ctx.enter_context(nc.semaphore(name))

        par = sb("par", [P, PARAMS["_all"][1]])
        con = sb("con", [P, CONSTS["_all"][1]])
        sel = sb("sel", [2 * EG, PAIRS, P], F16)
        ident16 = sb("ident16", [P, P], F16)
        ones16 = sb("ones16", [P, P], F16)
        wm = sb("wm", [P, PAIRS, 4 * GROUPS, P], F16)
        work = sb("work", [P, 6, BLK])
        decay_tab = sb("decay_tab", [P, HEADS, 3 * P])
        alpha = sb("alpha", [P, 4, HEADS])
        vb1t = sb("vb1t", [P, 3, 16])
        qb0s = sb("qb0s", [P, 4])
        b2h = sb("b2h", [P, P])
        xin = sb("xin", [P, TILES, P])
        xs = sb("xs", [P, TILES, P])
        xout = sb("xout", [P, TILES, P])
        xn = sb("xn", [P, TILES, P])
        xT = sb("xT", [P, NB, SEQ + 2 * PAD])
        stats = sb("stats", [P, TILES, 6])
        mv = sb("mv", [P, TILES, 2])
        vare = sb("vare", [P, TILES])
        rstd = sb("rstd", [P, TILES])
        xh = sb("xh", [P, BLK], F16)
        xl = sb("xl", [P, BLK], F16)
        big = sb("big", [P, 4, BLK])
        probs = big[:, 0:2, :].rearrange("p a n -> p (a n)")[:, 0:TILES * EXPERTS].rearrange("p (t e) -> p t e", t=TILES)
        rep = big[:, 2:4, :].rearrange("p a n -> p (a n)")[:, 0:TILES * EXPERTS].rearrange("p (t e) -> p t e", t=TILES)
        m8 = sb("m8", [P, TILES, TOPK])
        wsum = sb("wsum", [P, 3, TILES])
        comb = sb("comb", [P, TILES, SLOTS])
        comb16 = sb("comb16", [P, TILES * GROUPS, 2 * EG], F16)
        combT = sb("combT", [2 * EG, GROUPS, BLK], F16)
        shared = sb("shared", [P, 4, BLK])
        att = shared[:, 0, :].rearrange("p (t d) -> p t d", t=TILES)
        attT = shared[:, 1, :]
        yT = shared[:, 2, :]
        pf = big[:, 0:2, :]
        oT = big[:, 2:4, 0:SEQ]
        qst = sb("qst", [P, HG, BLK], F16)
        kst0 = sb("kst0", [P, HG, NB, SEQ], F16)
        hh = qst[:, 0:GROUPS, :]
        hl = kst0[:, 0:GROUPS, :, :].rearrange("p g b q -> p g (b q)")
        kst1 = sb("kst1", [P, 2, NB, SEQ + 2 * PAD], F16)
        va0 = sb("va0", [P, TILES, HEADS, HDP])
        va1 = sb("va1", [P, NB, 3, 2, HDP])
        nmax = sb("nmax", [P, 2, P])
        nmaxT = sb("nmaxT", [P, 2, SEQ], F16)
        rden = sb("rden", [P, 2, GRP * QT])
        odd = sb("odd", [4, NB, 2 * P])
        rank = shared[0:4, :, :].rearrange("p (b m) n -> p b m n", b=NB)
        weff = big[:, :, :].rearrange("p (b m) n -> p b m n", b=NB)
        hid = work[:, 0:4, :].rearrange("p (b r) (c q) -> p b (r c) q", b=NB, c=2)

        bank = [ctx.enter_context(nc.psum_tensor(f"bank{n}", [P, 512], F32)) for n in range(8)]
        b_xT = bank[0]

        def pc(name):
            a, w = PARAMS[name]
            return par[:, a:a + w]

        def cc(name, rows=P):
            a, w = CONSTS[name]
            return con[0:rows, a:a + w]

        ident = cc("ident")
        xT_mid = xT[:, :, PAD:PAD + SEQ]

        def xT_tile(t):
            return xT[:, t // QT, PAD + (t % QT) * P:PAD + (t % QT + 1) * P]

        params_in, consts_in, w_in = sem("params_in"), sem("consts_in"), [sem(f"w_in{r}") for r in range(3)]
        w_hi, w_lo = sem("w_hi"), sem("w_lo")
        setup_pool, setup_dve, setup_act, decay_ready = sem("setup_pool"), sem("setup_dve"), sem("setup_act"), sem("decay_ready")
        x_in, x_taken, out_ready, stored = sem("x_in"), sem("x_taken"), sem("out_ready"), sem("stored")
        dve_step, carried = sem("dve_step"), sem("carried")
        var_ready, rstd_ready = sem("var_ready"), sem("rstd_ready")
        xn_ready, xT_raw, xT_ready = sem("xn_ready"), sem("xT_raw"), sem("xT_ready")
        router_raw, logits_ready, probs_ready = sem("router_raw"), sem("logits_ready"), sem("probs_ready")
        x_split, comb_ready = sem("x_split"), sem("comb_ready")
        combT_raw, combT_ready = sem("combT_raw"), sem("combT_ready")
        gate_raw, spread_raw = sem("gate_raw"), sem("spread_raw")
        silu_done, weighted = sem("silu_done"), sem("weighted")
        h_hi, h_lo, h_used = sem("h_hi"), sem("h_lo"), sem("h_used")
        y_raw, y_copied, y_tok = sem("y_raw"), sem("y_copied"), sem("y_tok")
        proj_raw, proj_copied, stacked = sem("proj_raw"), sem("proj_copied"), sem("stacked")
        v_raw, v_ready = sem("v_raw"), sem("v_ready")
        scores_raw, maxed = sem("scores_raw"), sem("maxed")
        nmaxT_raw, nmaxT_ready = sem("nmaxT_raw"), sem("nmaxT_ready")
        keyside_raw, biased, exp_done = sem("keyside_raw"), sem("biased"), sem("exp_done")
        pv_done, oT_ready, turned, divided = sem("pv_done"), sem("oT_ready"), sem("turned"), sem("divided")
        attT_raw, attT_ready, out_raw = sem("attT_raw"), sem("attT_ready"), sem("out_raw")
        picked_raw, rank_ready, outer_raw, weff_ready = sem("picked_raw"), sem("rank_ready"), sem("outer_raw"), sem("weff_ready")
        hid_raw, hid_ready, down_raw = sem("hid_raw"), sem("hid_ready"), sem("down_raw")

        def stage(r):
            return work[:].rearrange("p a b -> p (a b)")[:, r * 1024:r * 1024 + 2 * GROUPS * P]

        def piece(m, r, lo):
            return wm[:, m * 3 + r, lo:4 * GROUPS:2, :]

        def spread_bank(g):
            return bank[(4, 5, 7)[g]]

        def y_done(i, u):
            return h_used, i * (2 * CHUNKS) + (u + 1) * CHUNKS

        block = ctx.enter_context(nc.Block())

        @block.sync
        def _(sp):
            sp.dma_start(par[:], params).then_inc(params_in, 16)
            sp.dma_start(con[:], consts).then_inc(consts_in, 16)
            sp.dma_start(xin[:], x_v[0]).then_inc(x_in, 16)
            for r in range(3):
                sp.dma_start(stage(r), wmoe[r]).then_inc(w_in[r], 16)
            sp.dma_start(sel[:], sel16[0:2 * EG, 0:PAIRS * P].rearrange("p (j m) -> p j m", m=P)).then_inc(consts_in, 16)
            sp.dma_start(ident16[:], sel16[:, PAIRS * P:(PAIRS + 1) * P]).then_inc(consts_in, 16)
            assert PAIRS % 3 == 0
            with sp.Fori(1, PAIRS // 3) as m:
                for r in range(3):
                    sp.wait_ge(w_hi, m * 3 + (r - 2))
                    sp.wait_ge(w_lo, m * 3 + (r - 2))
                    sp.dma_start(stage(r), wmoe[m * 3 + r]).then_inc(w_in[r], 16)
            with sp.Fori(0, BLOCKS - 1) as i:
                sp.wait_ge(x_taken, i + 1)
                sp.dma_start(xin[:], x_v[i + 1]).then_inc(x_in, 16)
                sp.wait_ge(out_ready, i + 1)
                sp.dma_start(out_v[i], xout[:]).then_inc(stored, 16)
            sp.wait_ge(out_ready, BLOCKS)
            sp.dma_start(out_v[BLOCKS - 1], xout[:]).then_inc(stored, 16)
            sp.wait_ge(stored, 16 * (BLOCKS + 1))

        @block.gpsimd
        def _(pool):
            nc.gpsimd.memset(xT[:], 0.0).then_inc(setup_pool, 1)
            nc.gpsimd.memset(kst1[:], 0.0).then_inc(setup_pool, 1)
            nc.gpsimd.memset(va0[:], 0.0).then_inc(setup_pool, 1)
            nc.gpsimd.memset(va1[:], 0.0).then_inc(setup_pool, 1)
            nc.gpsimd.memset(nmax[:], 0.0).then_inc(setup_pool, 1)
            nc.gpsimd.memset(ones16[:], 1.0).then_inc(setup_pool, 1)
            pool.wait_ge(setup_pool, 6)
            nc.gpsimd.memset(va0[:, :, :, HD:HD + 1], 1.0).then_inc(setup_pool, 1)
            nc.gpsimd.memset(va1[:, :, :, :, HD:HD + 1], 1.0).then_inc(setup_pool, 1)
            nc.gpsimd.memset(comb[:, :, EXPERTS:EXPERTS + 1], 1.0).then_inc(setup_pool, 1)
            nc.gpsimd.memset(comb[:, :, EXPERTS + 1:], 0.0).then_inc(setup_pool, 1)
            pool.wait_ge(consts_in, 48)
            pool.wait_ge(setup_dve, 5)
            for h in range(HEADS):
                nc.gpsimd.tensor_scalar(decay_tab[:, h, :], cc("negdist"), alpha[:, 3, h:h + 1], None,
                                        ALU.mult).then_inc(decay_ready, 1)
            with pool.Fori(0, BLOCKS) as i:
                for s in range(STAGES):
                    pool.wait_ge(var_ready, i * STAGES + (s + 1))
                    nc.gpsimd.tensor_tensor(rstd[:], vare[:], cc("pow"), ALU.pow).then_inc(rstd_ready, 1)

        @block.tensor
        def _(pe):
            pe.wait_ge(consts_in, 48)
            pe.wait_ge(params_in, 16)
            pe.wait_ge(setup_pool, 10)
            pe.wait_ge(w_hi, PAIRS)
            pe.wait_ge(w_lo, PAIRS)

            with pe.Fori(0, BLOCKS) as i:
                def transposes(s):
                    pe.wait_ge(xn_ready, i * STAGES + (s + 1))
                    for t in range(TILES):
                        mm = nc.tensor.transpose(b_xT[:, t * P:(t + 1) * P], xn[:, t, :], ident)
                    mm.then_inc(xT_raw, 1)
                    pe.wait_ge(xT_ready, i * STAGES + (s + 1))

                def moe(s, u):
                    transposes(s)
                    for t in range(TILES):
                        mm = nc.tensor.matmul(bank[1 + t // 2][:, (t % 2) * 256:(t % 2) * 256 + EXPERTS],
                                              xT_tile(t), pc("router"), start=True, stop=True)
                    mm.then_inc(router_raw, 1)
                    pe.wait_ge(comb_ready, i * 2 + (u + 1))
                    for g in range(GROUPS):
                        dst = bank[4 + g // 2][:, (g % 2) * 256:(g % 2 + 1) * 256].bitcast(F16)
                        for t in range(TILES):
                            mm = nc.tensor.transpose(dst[0:2 * EG, t * P:(t + 1) * P],
                                                     comb16[:, t * GROUPS + g, :], ident16[:, :])
                    mm.then_inc(combT_raw, 1)
                    pe.wait_ge(combT_ready, i * 2 + (u + 1))
                    pe.wait_ge(x_split, i * 2 + (u + 1))
                    n0 = pe.snap(i * (2 * CHUNKS) + u * CHUNKS)

                    def gate(j, g):
                        nc.tensor.matmul(bank[1 + g][:, :], wm[:, j, 4 * g, :], xh[:, :], start=True, stop=False)
                        nc.tensor.matmul(bank[1 + g][:, :], wm[:, j, 4 * g, :], xl[:, :], start=False, stop=False)
                        nc.tensor.matmul(bank[1 + g][:, :], wm[:, j, 4 * g + 1, :], xh[:, :],
                                         start=False, stop=True).then_inc(gate_raw, 1)

                    def spread(j, g):
                        nc.tensor.matmul(spread_bank(g)[:, :], sel[:, j, :], combT[:, g, :],
                                         start=True, stop=True).then_inc(spread_raw, 1)

                    def down(j, g, first, last):
                        nc.tensor.matmul(bank[6][:, :], wm[:, j, 4 * g + 2, :], hh[:, g, :],
                                         start=first, stop=False)
                        nc.tensor.matmul(bank[6][:, :], wm[:, j, 4 * g + 3, :], hh[:, g, :],
                                         start=False, stop=False)
                        nc.tensor.matmul(bank[6][:, :], wm[:, j, 4 * g + 2, :], hl[:, g, :],
                                         start=False, stop=last).then_inc(h_used, 1)

                    for g in range(GROUPS):
                        gate(0, g)
                        spread(0, g)

                    def steady(j, first):
                        n = pe.snap(n0 + j * GROUPS)
                        for g in range(GROUPS):
                            pe.wait_ge(silu_done, n + (g - 2))
                            gate(j, g)
                            pe.wait_ge(weighted, n + (g - 2))
                            spread(j, g)
                            pe.wait_ge(h_lo, n + (g - 2))
                            down(j - 1, g, first and g == 0, False)

                    steady(1, True)
                    with pe.Fori(2, PAIRS) as j:
                        steady(j, False)
                    for g in range(GROUPS):
                        pe.wait_ge(h_lo, n0 + (CHUNKS - GROUPS + g + 1))
                        down(PAIRS - 1, g, False, g == GROUPS - 1)
                    pe.wait_ge(y_copied, i * 2 + (u + 1))
                    for t in range(TILES):
                        mm = nc.tensor.transpose(b_xT[:, t * P:(t + 1) * P], yT[:, t * P:(t + 1) * P], ident)
                    mm.then_inc(y_tok, 1)

                def attention(s, a):
                    transposes(s)
                    wq = pc("qk0" if a == 0 else "qk1")
                    p0 = a * N_PROJ[0]
                    for n in range(N_PROJ[a]):
                        if n >= 3:
                            pe.wait_ge(proj_copied, i * PROJ + (p0 + n - 2))
                        nc.tensor.matmul(bank[1 + n % 3][:, :], wq[:, n * P:(n + 1) * P], xT_mid,
                                         start=True, stop=True).then_inc(proj_raw, 1)
                    if a == 0:
                        for t in range(TILES):
                            mm = nc.tensor.matmul(bank[7][:, t * P:(t + 1) * P], xT_tile(t), pc("v0"),
                                                  start=True, stop=True)
                    else:
                        for b in range(NB):
                            for g, (key0, _, _) in enumerate(SEGS[1]):
                                c = (b * 3 + g) * 16
                                mm = nc.tensor.matmul(bank[7][:, c:c + 16], xT[:, b, key0:key0 + P], pc("v1"),
                                                      start=True, stop=True)
                    mm.then_inc(v_raw, 1)
                    u0, g0 = a * UNITS, a * NGRP

                    def query_side(n):
                        b, h = n // HEADS, n % HEADS
                        rows = slice(32 * (h % 4), 32 * (h % 4) + 32)
                        if n >= 2:
                            pe.wait_ge(maxed, i * (2 * UNITS) + (u0 + n - 1))
                        for qt in range(QT):
                            lhs = qst[rows, h // 4, b * SEQ + qt * P:b * SEQ + (qt + 1) * P]
                            if a == 0:
                                rhs, keys = kst0[rows, h // 4, b, :], SEQ
                            else:
                                rhs, keys = kst1[rows, h // 8, b, qt * P:qt * P + W1KEYS], W1KEYS
                            mm = nc.tensor.matmul(bank[1 + n % 2][:, qt * 256:qt * 256 + keys], lhs, rhs,
                                                  start=True, stop=True)
                        mm.then_inc(scores_raw, 1)

                    def turn_maxima(k):
                        pe.wait_ge(maxed, i * (2 * UNITS) + (u0 + GRP * (k + 1)))
                        if k >= 1:
                            pe.wait_ge(nmaxT_ready, i * (2 * NGRP) + (g0 + k))
                        nc.tensor.transpose(bank[7][:, 0:P], nmax[:, k % 2, :], ident).then_inc(nmaxT_raw, 1)

                    def key_side(n):
                        b, h = n // HEADS, n % HEADS
                        rows = slice(32 * (h % 4), 32 * (h % 4) + 32)
                        if n % GRP == 0:
                            pe.wait_ge(nmaxT_ready, i * (2 * NGRP) + (g0 + n // GRP + 1))
                        if n >= 2:
                            pe.wait_ge(biased, i * (2 * UNITS) + (u0 + n - 1))
                        c = 0
                        for g, (key0, q0, nq) in enumerate(SEGS[a]):
                            dst = bank[3 + n % 2][:, c:c + nq]
                            keys = kst0[rows, h // 4, b, key0:key0 + P] if a == 0 else                                 kst1[rows, h // 8, b, key0:key0 + P]
                            nc.tensor.matmul(dst, ones16[rows, :], nmaxT[rows, n // GRP % 2, q0:q0 + nq],
                                             start=(g == 0), stop=False, skip_group_check=True)
                            mm = nc.tensor.matmul(dst, keys, qst[rows, h // 4, b * SEQ + q0:b * SEQ + q0 + nq],
                                                  start=False, stop=True, skip_group_check=True)
                            c += nq
                        mm.then_inc(keyside_raw, 1)

                    def values(n):
                        b, h, k = n // HEADS, n % HEADS, n // GRP
                        pe.wait_ge(exp_done, i * (2 * UNITS) + (u0 + n + 1))
                        if n % GRP == 0 and k >= 2:
                            pe.wait_ge(oT_ready, i * (2 * NGRP) + (g0 + k - 1))
                        r, c = HDP * (n % GRP), 0
                        for g, (key0, q0, nq) in enumerate(SEGS[a]):
                            v = va0[:, b * QT + key0 // P, h, :] if a == 0 else va1[:, b, g, h // 8, :]
                            mm = nc.tensor.matmul(bank[5 + k % 2][r:r + HDP, q0:q0 + nq], v,
                                                  work[:, 2 + n % 2, c:c + nq], start=(g == 0),
                                                  stop=(g == len(SEGS[a]) - 1), skip_group_check=True)
                            c += nq
                        mm.then_inc(pv_done, 1)

                    def turn_back(k):
                        pe.wait_ge(oT_ready, i * (2 * NGRP) + (g0 + k + 1))
                        if k >= 1:
                            pe.wait_ge(divided, i * (2 * NGRP) + (g0 + k))
                        for qt in range(QT):
                            mm = nc.tensor.transpose(bank[0][:, qt * P:(qt + 1) * P],
                                                     oT[:, k % 2, qt * P:(qt + 1) * P], ident)
                        mm.then_inc(turned, 1)

                    pe.wait_ge(stacked, i * PROJ + (p0 + N_PROJ[a]))
                    for slot in range(SLOTS_A):
                        if slot < UNITS:
                            query_side(slot)
                        if slot == 1:
                            pe.wait_ge(v_ready, i * 2 + (a + 1))
                        if slot % GRP == 0 and 1 <= slot // GRP <= NGRP:
                            turn_maxima(slot // GRP - 1)
                        if 0 <= slot - LK < UNITS:
                            key_side(slot - LK)
                        if 0 <= slot - LV < UNITS:
                            values(slot - LV)
                        if (slot - LB) % GRP == 0 and 0 <= (slot - LB) // GRP < NGRP:
                            turn_back((slot - LB) // GRP)
                    pe.wait_ge(divided, i * (2 * NGRP) + (g0 + NGRP))
                    for t in range(TILES):
                        mm = nc.tensor.transpose(bank[1][:, t * P:(t + 1) * P], att[:, t, :], ident)
                    mm.then_inc(attT_raw, 1)
                    pe.wait_ge(attT_ready, i * 2 + (a + 1))
                    for t in range(TILES):
                        mm = nc.tensor.matmul(bank[2][:, t * P:(t + 1) * P], attT[:, t * P:(t + 1) * P],
                                              pc("o0" if a == 0 else "o1"), start=True, stop=True)
                    mm.then_inc(out_raw, 1)

                def ffn(s, u):
                    transposes(s)
                    for b in range(NB):
                        if b == 1:
                            pe.wait_ge(rank_ready, i * 4 + (2 * u + b))
                        rows = xn[:, b * QT, :]
                        nc.tensor.matmul(bank[1][0:4, 0:P], cc("selO1"), rows, start=True, stop=True)
                        nc.tensor.matmul(bank[1][0:4, P:2 * P], cc("selO2"), rows, start=True, stop=True)
                        nc.tensor.matmul(bank[2][0:4, :], cc("selE1"),
                                         rows.unsqueeze(1).broadcast_to([P, 4, P]), start=True, stop=True)
                        for r in range(HJ):
                            mm = nc.tensor.matmul(bank[3][0:4, r * P:(r + 1) * P], cc("selE2"),
                                                  rows.rearrange("p (q r) -> p r q", r=4)[:, r, :].unsqueeze(1)
                                                  .broadcast_to([P, 4, 32]), start=True, stop=True)
                        mm.then_inc(picked_raw, 1)
                    for b in range(NB):
                        if b == 1:
                            pe.wait_ge(weff_ready, i * 4 + (2 * u + b))
                        pe.wait_ge(rank_ready, i * 4 + (2 * u + b + 1))
                        for m in range(2):
                            mm = nc.tensor.matmul(bank[4 + m][:, :], odd[:, b, m * P:(m + 1) * P],
                                                  rank[:, b, m, :], start=True, stop=True)
                        mm.then_inc(outer_raw, 1)
                    for b in range(NB):
                        pe.wait_ge(weff_ready, i * 4 + (2 * u + b + 1))
                        for half in range(2):
                            if b == 1:
                                pe.wait_ge(hid_ready, i * 8 + (4 * u + half + 1))
                            for jj in range(2):
                                j = 2 * half + jj
                                mm = nc.tensor.matmul(bank[6 + half][:, jj * SEQ:(jj + 1) * SEQ],
                                                      weff[:, b, 0, j * P:(j + 1) * P], xT_mid[:, b, :],
                                                      start=True, stop=True)
                            mm.then_inc(hid_raw, 1)
                    for b in range(NB):
                        pe.wait_ge(hid_ready, i * 8 + (4 * u + 2 * b + 2))
                        for tt in range(QT):
                            t = b * QT + tt
                            for r in range(HJ):
                                mm = nc.tensor.matmul(b_xT[:, t * P:(t + 1) * P],
                                                      hid[:, b, r, tt * P:(tt + 1) * P],
                                                      weff[:, b, 1, r * P:(r + 1) * P],
                                                      start=(r == 0), stop=(r == HJ - 1))
                    mm.then_inc(down_raw, 1)

                moe(0, 0)
                attention(1, 0)
                moe(2, 1)
                ffn(3, 0)
                attention(4, 1)
                ffn(5, 1)

        @block.scalar
        def _(act):
            act.wait_ge(setup_dve, 1)
            nc.scalar.activation(alpha[:, 1, :], alpha[:, 0, :], ACT.Exp, scale=-1.0).then_inc(setup_act, 1)
            act.wait_ge(setup_act, 1)
            nc.scalar.activation(alpha[:, 2, :], alpha[:, 1, :], ACT.Ln, bias=1.0).then_inc(setup_act, 1)
            with act.Fori(0, PAIRS // 3) as m:
                for r in range(3):
                    act.wait_ge(w_in[r], m * 16 + 16)
                    nc.scalar.copy(piece(m, r, 0), stage(r).rearrange("p (c n) -> p c n", n=P)).then_inc(w_hi, 1)

            with act.Fori(0, BLOCKS) as i:
                def copy_xT(s):
                    act.wait_ge(xT_raw, i * STAGES + (s + 1))
                    nc.scalar.copy(xT_mid, b_xT[:, :].rearrange("p (b q) -> p b q", b=NB)).then_inc(xT_ready, 1)

                def moe(s, u):
                    copy_xT(s)
                    act.wait_ge(logits_ready, i * 2 + (u + 1))
                    nc.scalar.activation(probs[:], rep[:], ACT.Sigmoid).then_inc(probs_ready, 1)
                    act.wait_ge(combT_raw, i * 2 + (u + 1))
                    nc.scalar.copy(combT[:, 0:2, :], bank[4][0:2 * EG, :].bitcast(F16)
                                   .rearrange("p (g n) -> p g n", g=2))
                    nc.scalar.copy(combT[:, 2, :], bank[5][0:2 * EG, 0:256].bitcast(F16)).then_inc(combT_ready, 1)
                    n0 = act.snap(i * (2 * CHUNKS) + u * CHUNKS)

                    def silu(n, g, first):
                        act.wait_ge(gate_raw, n + (g + 1))
                        if not first:
                            act.wait_ge(weighted, n + (g - 2))
                        nc.scalar.activation(work[:, g, :], bank[1 + g][:, :], ACT.Silu).then_inc(silu_done, 1)

                    def high(n, g, first):
                        act.wait_ge(weighted, n + (g + 1))
                        if not first:
                            act.wait_ge(h_used, n + (g - 2))
                        nc.scalar.copy(hh[:, g, :], work[:, 3 + g, :]).then_inc(h_hi, 1)

                    silu(n0, 0, True)
                    silu(n0, 1, True)
                    high(n0, 0, True)
                    silu(n0, 2, True)
                    high(n0, 1, True)

                    def steady(j, first):
                        n = act.snap(n0 + j * GROUPS)
                        silu(n, 0, False)
                        high(n + (-GROUPS), 2, first)
                        silu(n, 1, False)
                        high(n, 0, False)
                        silu(n, 2, False)
                        high(n, 1, False)

                    steady(1, True)
                    with act.Fori(2, PAIRS) as j:
                        steady(j, False)
                    high(n0 + (CHUNKS - GROUPS), 2, False)
                    act.wait_ge(y_done(i, u)[0], y_done(i, u)[1])
                    nc.scalar.copy(yT[:, :], bank[6][:, :]).then_inc(y_copied, 1)

                def attention(s, a):
                    copy_xT(s)
                    p0, u0, g0 = a * N_PROJ[0], a * UNITS, a * NGRP
                    for n in range(N_PROJ[a]):
                        act.wait_ge(proj_raw, i * PROJ + (p0 + n + 1))
                        if n >= 2:
                            act.wait_ge(stacked, i * PROJ + (p0 + n - 1))
                        if n < HG:
                            bias = qb0s[:, n:n + 1] if a == 0 else pc("qb1")[:, n:n + 1]
                            scale = HD ** -0.5 if a == 0 else 1.0
                        else:
                            bias, scale = pc("kb0" if a == 0 else "kb1")[:, n - HG:n - HG + 1], 1.0
                        nc.scalar.activation(pf[:, n % 2, :], bank[1 + n % 3][:, :], ACT.Identity,
                                             bias=bias, scale=scale).then_inc(proj_copied, 1)
                    def spread_maxima(k):
                        act.wait_ge(nmaxT_raw, i * (2 * NGRP) + (g0 + k + 1))
                        for qt in range(QT):
                            ins = nc.scalar.mul(nmaxT[:, k % 2, qt * P:(qt + 1) * P], bank[7][:, 0:P],
                                                cc("half")[:, qt:qt + 1])
                        ins.then_inc(nmaxT_ready, 1)

                    def exponent(n):
                        act.wait_ge(biased, i * (2 * UNITS) + (u0 + n + 1))
                        if n >= 2:
                            act.wait_ge(pv_done, i * (2 * UNITS) + (u0 + n - 1))
                        nc.scalar.activation(work[:, 2 + n % 2, 0:COLS[a]], work[:, n % 2, 0:COLS[a]],
                                             ACT.Exp).then_inc(exp_done, 1)

                    def copy_oT(k):
                        act.wait_ge(pv_done, i * (2 * UNITS) + (u0 + GRP * (k + 1)))
                        if k >= 2:
                            act.wait_ge(turned, i * (2 * NGRP) + (g0 + k - 1))
                        nc.scalar.copy(oT[:, k % 2, :], bank[5 + k % 2][:, 0:SEQ]).then_inc(oT_ready, 1)

                    for slot in range(SLOTS_A):
                        if slot % GRP == 0 and 1 <= slot // GRP <= NGRP:
                            spread_maxima(slot // GRP - 1)
                        if 0 <= slot - LK < UNITS:
                            exponent(slot - LK)
                        if (slot - LC) % GRP == 0 and 0 <= (slot - LC) // GRP < NGRP:
                            copy_oT((slot - LC) // GRP)
                    act.wait_ge(attT_raw, i * 2 + (a + 1))
                    nc.scalar.copy(attT[:, :], bank[1][:, :]).then_inc(attT_ready, 1)

                def ffn(s, u):
                    copy_xT(s)
                    for b in range(NB):
                        for half in range(2):
                            act.wait_ge(hid_raw, i * 8 + (4 * u + 2 * b + half + 1))
                            for jj in range(2):
                                j = 2 * half + jj
                                ins = nc.scalar.activation(hid[:, b, j, :], bank[6 + half][:, jj * SEQ:(jj + 1) * SEQ],
                                                           ACT.Gelu, bias=pc("b1")[:, j:j + 1])
                            ins.then_inc(hid_ready, 1)

                moe(0, 0)
                attention(1, 0)
                moe(2, 1)
                ffn(3, 0)
                attention(4, 1)
                ffn(5, 1)

        @block.vector
        def _(dve):
            dve.wait_ge(params_in, 16)
            dve.wait_ge(consts_in, 48)
            nc.vector.scalar_tensor_tensor(out=alpha[:, 0, :], in0=pc("decay"), scalar=-1.0, in1=pc("decay"),
                                           op0=ALU.mult, op1=ALU.max).then_inc(setup_dve, 1)
            nc.vector.tensor_scalar(qb0s[:], pc("qb0"), HD ** -0.5, None, ALU.mult).then_inc(setup_dve, 1)
            nc.vector.tensor_scalar(b2h[:], pc("b2"), 0.5, None, ALU.mult).then_inc(setup_dve, 1)
            nc.vector.tensor_tensor(vb1t[:], pc("vb1").unsqueeze(1).broadcast_to([P, 3, 16]),
                                    cc("valid").unsqueeze(2).broadcast_to([P, 3, 16]),
                                    ALU.mult).then_inc(setup_dve, 1)
            dve.wait_ge(setup_act, 2)
            nc.vector.scalar_tensor_tensor(out=alpha[:, 3, :], in0=pc("decay"), scalar=0.0, in1=alpha[:, 2, :],
                                           op0=ALU.max, op1=ALU.add).then_inc(setup_dve, 1)
            with dve.Fori(0, PAIRS // 3) as m:
                for r in range(3):
                    dve.wait_ge(w_in[r], m * 16 + 16)
                    dve.wait_ge(w_hi, m * 3 + (r + 1))
                    nc.vector.tensor_tensor(piece(m, r, 1), stage(r).rearrange("p (c n) -> p c n", n=P),
                                            piece(m, r, 0), ALU.subtract).then_inc(w_lo, 1)
            nc.vector.memset(xout[:], 0.0).then_inc(stored, 16)
            dve.wait_ge(stored, 16)
            dve.wait_ge(setup_pool, 10)
            dve.wait_ge(setup_dve, 5)
            dve.wait_ge(decay_ready, HEADS)

            with dve.Fori(0, BLOCKS) as i:
                steps = [0]

                def settle(ins, plain=False):
                    steps[0] += 1
                    ins.then_inc(dve_step, 1)
                    dve.wait_ge(dve_step, i * DVE_STEPS + steps[0])
                    if plain:
                        plain_wait()

                def plain_wait():
                    dve.sem_inc(carried, 1)

                def layer_norm(s):
                    for t in range(TILES):
                        ins = nc.vector.bn_stats(stats[:, t, :], xs[:, t, :])
                    settle(ins, plain=True)
                    for t in range(TILES):
                        ins = nc.vector.bn_aggr(mv[:, t, :], stats[:, t, :])
                    settle(ins)
                    nc.vector.tensor_scalar(vare[:], mv[:, :, 1], EPS, None, ALU.add).then_inc(var_ready, 1)
                    dve.wait_ge(rstd_ready, i * STAGES + (s + 1))
                    for t in range(TILES):
                        ins = nc.vector.tensor_scalar(xn[:, t, :], xs[:, t, :], mv[:, t, 0:1], rstd[:, t:t + 1],
                                                      ALU.subtract, ALU.mult)
                    ins.then_inc(xn_ready, 1)

                def moe(s, u):
                    layer_norm(s)
                    dve.wait_ge(xT_ready, i * STAGES + (s + 1))
                    xh_v = xh[:, :].rearrange("p (b q) -> p b q", b=NB)
                    settle(nc.vector.tensor_copy(xh_v, xT_mid))
                    nc.vector.tensor_tensor(xl[:, :].rearrange("p (b q) -> p b q", b=NB), xT_mid, xh_v,
                                            ALU.subtract).then_inc(x_split, 1)
                    dve.wait_ge(router_raw, i * 2 + (u + 1))
                    for k in range(2):
                        ins = nc.vector.tensor_tensor(
                            rep[:, 2 * k:2 * k + 2, :],
                            bank[1 + k][:, :].rearrange("p (t e) -> p t e", t=2)[:, :, 0:EXPERTS],
                            pc("ebias").unsqueeze(1).broadcast_to([P, 2, EXPERTS]), ALU.add)
                    ins.then_inc(logits_ready, 1)
                    dve.wait_ge(probs_ready, i * 2 + (u + 1))
                    plain_wait()
                    for t in range(TILES):
                        ins = nc.vector.max(m8[:, t, :], probs[:, t, :])
                    settle(ins, plain=True)
                    for t in range(TILES):
                        ins = nc.vector.match_replace(rep[:, t, :], m8[:, t, :], probs[:, t, :], -1.0)
                    settle(nc.vector.tensor_reduce(wsum[:, 0, :], m8[:], AX.X, ALU.add))
                    settle(nc.vector.tensor_scalar(wsum[:, 1, :], wsum[:, 0, :], 1e-9, None, ALU.add))
                    settle(nc.vector.reciprocal(wsum[:, 2, :], wsum[:, 1, :]))
                    settle(nc.vector.tensor_scalar(wsum[:, 0, :], wsum[:, 2, :], ROUTED_SCALE, None, ALU.mult))
                    settle(nc.vector.scalar_tensor_tensor(out=rep[:], in0=rep[:], scalar=0.0, in1=probs[:],
                                                          op0=ALU.is_lt, op1=ALU.mult))
                    settle(nc.vector.tensor_tensor(comb[:, :, 0:EXPERTS], rep[:],
                                                   wsum[:, 0, :].unsqueeze(2).broadcast_to([P, TILES, EXPERTS]),
                                                   ALU.mult))
                    comb_v = comb[:].rearrange("p t (g e) -> p (t g) e", g=GROUPS)
                    settle(nc.vector.tensor_copy(comb16[:, :, 0:EG], comb_v))
                    nc.vector.tensor_tensor(comb16[:, :, EG:], comb_v, comb16[:, :, 0:EG],
                                            ALU.subtract).then_inc(comb_ready, 1)
                    n0 = dve.snap(i * (2 * CHUNKS) + u * CHUNKS)

                    def weigh(n, g, first=False):
                        if not first:
                            dve.wait_ge(h_lo, n + (g - 2))
                        dve.wait_ge(silu_done, n + (g + 1))
                        dve.wait_ge(spread_raw, n + (g + 1))
                        nc.vector.tensor_tensor(work[:, 3 + g, :], work[:, g, :], spread_bank(g)[:, :],
                                                ALU.mult).then_inc(weighted, 1)

                    def low(n, g):
                        dve.wait_ge(h_hi, n + (g + 1))
                        nc.vector.tensor_tensor(hl[:, g, :], work[:, 3 + g, :], hh[:, g, :],
                                                ALU.subtract).then_inc(h_lo, 1)

                    weigh(n0, 0, True)
                    weigh(n0, 1, True)
                    low(n0, 0)
                    weigh(n0, 2, True)
                    low(n0, 1)
                    with dve.Fori(1, PAIRS) as j:
                        n = dve.snap(n0 + j * GROUPS)
                        weigh(n, 0)
                        low(n + (-GROUPS), 2)
                        weigh(n, 1)
                        low(n, 0)
                        weigh(n, 2)
                        low(n, 1)
                    low(n0 + (CHUNKS - GROUPS), 2)
                    dve.wait_ge(y_tok, i * 2 + (u + 1))
                    settle(nc.vector.scalar_tensor_tensor(out=xs[:], in0=tiles_of(b_xT), scalar=0.5, in1=xs[:],
                                                          op0=ALU.mult, op1=ALU.add))

                def attention(s, a):
                    layer_norm(s)
                    p0, u0, g0 = a * N_PROJ[0], a * UNITS, a * NGRP
                    for n in range(N_PROJ[a]):
                        phi = (xh, xl)[n % 2]
                        if n >= 2:
                            dve.wait_ge(stacked, i * PROJ + (p0 + n - 1))
                        dve.wait_ge(proj_copied, i * PROJ + (p0 + n + 1))
                        settle(nc.vector.tensor_copy(phi[:, :], pf[:, n % 2, :]))
                        if n < HG:
                            dst, mask = qst[:, n, :].rearrange("p (b q) -> p b q", b=NB), cc("mq")
                        elif a == 0:
                            dst, mask = kst0[:, n - HG, :, :], cc("mk")
                        else:
                            dst, mask = kst1[:, n - HG, :, PAD:PAD + SEQ], cc("mk")
                        nc.vector.scalar_tensor_tensor(
                            out=dst, in0=phi[:, :].rearrange("p (b q) -> p b q", b=NB), scalar=mask,
                            in1=pf[:, n % 2, :].rearrange("p (b q) -> p b q", b=NB),
                            op0=ALU.mult, op1=ALU.add).then_inc(stacked, 1)
                    dve.wait_ge(v_raw, i * 2 + (a + 1))
                    if a == 0:
                        for t in range(TILES):
                            ins = nc.vector.tensor_tensor(
                                va0[:, t, :, 0:HD], bank[7][:, t * P:(t + 1) * P].rearrange("p (h d) -> p h d", d=HD),
                                pc("vb0").rearrange("p (h d) -> p h d", d=HD), ALU.add)
                    else:
                        for b in range(NB):
                            ins = nc.vector.tensor_tensor(
                                va1[:, b, :, :, :].rearrange("p g k e -> p (g k) e")[:, :, 0:HD],
                                bank[7][:, b * 48:(b + 1) * 48].rearrange("p (c d) -> p c d", d=HD),
                                vb1t[:].rearrange("p g (k d) -> p (g k) d", d=HD), ALU.add)
                    ins.then_inc(v_ready, 1)

                    def maximum(n):
                        h, k = n % HEADS, n // GRP
                        if n >= 2:
                            dve.wait_ge(maxed, i * (2 * UNITS) + (u0 + n - 1))
                        dve.wait_ge(scores_raw, i * (2 * UNITS) + (u0 + n + 1))
                        plain_wait()
                        for qt in range(QT):
                            if a == 0:
                                keys, table = SEQ, decay_tab[:, h, (1 - qt) * P:(3 - qt) * P]
                            else:
                                keys, table = W1KEYS, cc("band")
                            c = 32 * (n % GRP) + qt
                            ins = nc.vector.tensor_tensor_reduce(
                                out=work[:, 4 + n % 2, qt * 256:qt * 256 + keys],
                                in0=bank[1 + n % 2][:, qt * 256:qt * 256 + keys], in1=table,
                                scale=-1.0, scalar=3e38, op0=ALU.add, op1=ALU.min,
                                accum_out=nmax[:, k % 2, c:c + 1])
                        ins.then_inc(maxed, 1)

                    def add_bias(n):
                        h = n % HEADS
                        if n >= 2:
                            dve.wait_ge(exp_done, i * (2 * UNITS) + (u0 + n - 1))
                        dve.wait_ge(keyside_raw, i * (2 * UNITS) + (u0 + n + 1))
                        if a == 0:
                            for g in range(2):
                                ins = nc.vector.tensor_tensor(work[:, n % 2, g * SEQ:(g + 1) * SEQ],
                                                              bank[3 + n % 2][:, g * SEQ:(g + 1) * SEQ],
                                                              decay_tab[:, h, g * P:g * P + SEQ], ALU.add)
                        else:
                            ins = nc.vector.tensor_tensor(work[:, n % 2, 0:COLS[1]], bank[3 + n % 2][:, 0:COLS[1]],
                                                          cc("bandT"), ALU.add)
                        ins.then_inc(biased, 1)

                    def divide(k):
                        b, hg = k // HG, k % HG
                        dve.wait_ge(turned, i * (2 * NGRP) + (g0 + k + 1))
                        o = bank[0][:, 0:SEQ].rearrange("p (c e) -> p c e", e=HDP)
                        settle(nc.vector.reciprocal(rden[:, k % 2, :], o[:, :, HD]))
                        o4 = bank[0][:, 0:SEQ].rearrange("p (t h e) -> p t h e", t=QT, e=HDP)[:, :, :, 0:HD]
                        r4 = rden[:, k % 2, :].rearrange("p (t h) -> p t h", t=QT).unsqueeze(3) \
                            .broadcast_to([P, QT, GRP, HD])
                        nc.vector.tensor_tensor(
                            att[:, b * QT:(b + 1) * QT, hg * GRP * HD:(hg + 1) * GRP * HD]
                            .rearrange("p t (h d) -> p t h d", d=HD), o4, r4, ALU.mult).then_inc(divided, 1)

                    for slot in range(SLOTS_A):
                        if slot < UNITS:
                            maximum(slot)
                        if 0 <= slot - LK < UNITS:
                            add_bias(slot - LK)
                        if (slot - LN) % GRP == 0 and 0 <= (slot - LN) // GRP < NGRP:
                            divide((slot - LN) // GRP)
                    dve.wait_ge(out_raw, i * 2 + (a + 1))
                    settle(nc.vector.tensor_tensor(xs[:], tiles_of(bank[2]), xs[:], ALU.add))
                    settle(nc.vector.tensor_tensor(xs[:], xs[:], pc("ob0" if a == 0 else "ob1").unsqueeze(1)
                                                   .broadcast_to([P, TILES, P]), ALU.add))

                def ffn(s, u):
                    layer_norm(s)
                    for b in range(NB):
                        dve.wait_ge(picked_raw, i * 4 + (2 * u + b + 1))
                        nc.vector.tensor_copy(odd[:, b, :], bank[1][0:4, 0:2 * P])
                        nc.vector.tensor_tensor(rank[:, b, 0, :].rearrange("p (j q) -> p j q", j=4),
                                                bank[2][0:4, :].rearrange("p (j q) -> p j q", j=4),
                                                cc("diag", 4).unsqueeze(2).broadcast_to([4, 4, P]), ALU.mult)
                        diag2 = cc("diag", 4).unsqueeze(2).broadcast_to([4, 4, 32])
                        for r in range(HJ):
                            ins = nc.vector.tensor_tensor(
                                rank[:, b, 1, r * P:(r + 1) * P].rearrange("p (j q) -> p j q", j=4),
                                bank[3][0:4, r * P:(r + 1) * P].rearrange("p (j q) -> p j q", j=4), diag2, ALU.mult)
                        ins.then_inc(rank_ready, 1)
                    for b in range(NB):
                        dve.wait_ge(outer_raw, i * 4 + (2 * u + b + 1))
                        for m, w in enumerate(("w1", "w2")):
                            ins = nc.vector.scalar_tensor_tensor(out=weff[:, b, m, :], in0=bank[4 + m][:, :],
                                                                 scalar=pc("scale"), in1=pc(w),
                                                                 op0=ALU.mult, op1=ALU.add)
                        ins.then_inc(weff_ready, 1)
                    dve.wait_ge(down_raw, i * 2 + (u + 1))
                    settle(nc.vector.scalar_tensor_tensor(out=xs[:], in0=tiles_of(b_xT), scalar=0.5, in1=xs[:],
                                                          op0=ALU.mult, op1=ALU.add))
                    b2_v = b2h[:].unsqueeze(1).broadcast_to([P, TILES, P])
                    if u == 0:
                        settle(nc.vector.tensor_tensor(xs[:], xs[:], b2_v, ALU.add))
                    else:
                        dve.wait_ge(stored, i * 16 + 16)
                        nc.vector.tensor_tensor(xout[:], xs[:], b2_v, ALU.add).then_inc(out_ready, 1)
                        dve.wait_ge(out_ready, i + 1)

                dve.wait_ge(x_in, i * 16 + 16)
                nc.vector.tensor_copy(xs[:], xin[:]).then_inc(x_taken, 1)
                dve.wait_ge(x_taken, i + 1)
                moe(0, 0)
                attention(1, 0)
                moe(2, 1)
                ffn(3, 0)
                attention(4, 1)
                ffn(5, 1)
                assert steps[0] == DVE_STEPS, steps[0]


def tiles_of(b):
    return b[:, :].rearrange("p (t d) -> p t d", t=TILES)


def lay_out(a):
    f = np.float32

    def rows(v):
        v = np.asarray(v, f).reshape(-1)
        return np.broadcast_to(v, (P, v.size))

    heads = np.array([[(4 * g + hh) * HD + d for hh in range(4) for c in range(4) for d in range(HD)]
                      for g in range(HG)])
    kv = np.array([[k * HD + d for hh in range(4) for c in range(4) for d in range(HD)] for k in range(2)])

    def stacks(w_cols, index):
        return np.concatenate([w_cols[:, ix] for ix in index], axis=1)

    qkv_wT, qkv_b = np.asarray(a["L0_attn_qkv_w"]).T, np.asarray(a["L0_attn_qkv_b"])
    values = {
        "router": np.asarray(a["L0_ffn_router_w"]).T, "ebias": rows(a["L0_ffn_expert_bias"]),
        "decay": rows(a["L0_attn_decay_alpha"]),
        "qk0": np.concatenate([stacks(qkv_wT[:, 0:D], heads), stacks(qkv_wT[:, D:2 * D], heads)], axis=1),
        "qb0": qkv_b[0:D][heads].T, "kb0": qkv_b[D:2 * D][heads].T,
        "v0": qkv_wT[:, 2 * D:], "vb0": rows(qkv_b[2 * D:]),
        "o0": np.asarray(a["L0_attn_out_w"]).T, "ob0": rows(a["L0_attn_out_b"]),
        "qk1": np.concatenate([stacks(np.asarray(a["L1_attn_Wq"]), heads), stacks(np.asarray(a["L1_attn_Wk"]), kv)], axis=1),
        "qb1": np.asarray(a["L1_attn_bq"])[heads].T, "kb1": np.asarray(a["L1_attn_bk"])[kv].T,
        "v1": np.asarray(a["L1_attn_Wv"]), "vb1": rows(a["L1_attn_bv"]),
        "o1": np.asarray(a["L1_attn_Wo"]), "ob1": rows(a["L1_attn_bo"]),
        "w1": np.asarray(a["L1_ffn_W1"]).T, "b1": np.asarray(a["L1_ffn_b1"]).reshape(HJ, P).T,
        "w2": np.asarray(a["L1_ffn_W2"]).T.reshape(HJ, P, D).transpose(1, 0, 2).reshape(P, HJ * D),
        "b2": rows(a["L1_ffn_b2"]), "scale": rows(a["L1_ffn_scale"]),
    }
    params = np.zeros((P, PARAMS["_all"][1]), f)
    for name, v in values.items():
        at, w = PARAMS[name]
        assert v.shape == (P, w), (name, v.shape)
        params[:, at:at + w] = v

    gate = np.concatenate([np.asarray(a["L0_ffn_w_gate"]), np.asarray(a["L0_ffn_w_gate_shared"])[None],
                           np.zeros((1, INTER, D), f)])
    down = np.concatenate([np.asarray(a["L0_ffn_w_down"]), np.asarray(a["L0_ffn_w_down_shared"])[None],
                           np.zeros((1, D, INTER), f)])
    gate = gate.reshape(GROUPS, PAIRS, P, D).transpose(1, 3, 0, 2)
    down = down.transpose(0, 2, 1).reshape(GROUPS, PAIRS, P, D).transpose(1, 2, 0, 3)
    wmoe = np.ascontiguousarray(np.stack([gate, down], axis=3)).reshape(PAIRS, P, 2 * GROUPS * P)
    return params, wmoe


def shape_constants():
    f = np.float32
    p = np.arange(P)
    values = {
        "ident": np.eye(P, dtype=f),
        "negdist": -np.abs(np.arange(3 * P)[None] - P - p[:, None]).astype(f),
        "band": np.where((np.arange(W1KEYS)[None] >= p[:, None]) & (np.arange(W1KEYS)[None] < p[:, None] + 2 * PAD),
                         0.0, NEG).astype(f),
        "mq": np.where(p % 32 >= 16, -1.0, 0.0).astype(f)[:, None],
        "mk": np.where(p % 16 >= 8, -1.0, 0.0).astype(f)[:, None],
        "bandT": np.concatenate([np.where((k0 + p[:, None] >= q0 + np.arange(nq)[None])
                                          & (k0 + p[:, None] < q0 + np.arange(nq)[None] + 2 * PAD)
                                          & (k0 + p[:, None] >= floor), 0.0, NEG)
                                 for (k0, q0, nq), floor in zip(SEGS[1], (0, P, SEQ))], 1).astype(f),
        "valid": np.stack([(k0 + p >= PAD) & (k0 + p < PAD + SEQ) for k0, _, _ in SEGS[1]], 1).astype(f),
        "half": (p[:, None] % QT == np.arange(QT)[None]).astype(f),
        "pow": np.full((P, TILES), -0.5, f),
        "diag": (p[:, None] == np.arange(4)[None]).astype(f),
    }
    for name, first in (("selE1", 1), ("selO1", 2), ("selE2", 9), ("selO2", 10)):
        values[name] = (p[:, None] == first + 2 * np.arange(4)[None]).astype(f)
    consts = np.zeros((P, CONSTS["_all"][1]), f)
    for name, v in values.items():
        at, w = CONSTS[name]
        assert v.shape == (P, w), (name, v.shape)
        consts[:, at:at + w] = v
    sel16 = np.zeros((P, (PAIRS + 1) * P), np.float16)
    for j in range(PAIRS):
        for m in range(P):
            sel16[2 * j + m // INTER, j * P + m] = 1
            sel16[EG + 2 * j + m // INTER, j * P + m] = 1
    sel16[:, PAIRS * P:(PAIRS + 1) * P] = np.eye(P)
    return consts, sel16


def kernel(**inputs):
    import numpy as _np
    import concourse.bacc as _bacc
    from concourse import mybir as _mybir
    from concourse.bass_utils import run_bass_kernel_spmd as _run

    params, wmoe = lay_out(inputs)
    consts, sel16 = shape_constants()
    nc = _bacc.Bacc("TRN2", target_bir_lowering=False, num_devices=1)
    arrays = {"x": _np.ascontiguousarray(inputs["L0_attn_x"]), "params": params, "consts": consts,
              "sel16": sel16, "wmoe": wmoe}
    args = [nc.dram_tensor(name, v.shape, _mybir.dt.from_np(v.dtype), kind="ExternalInput").ap()
            for name, v in arrays.items()]
    out = nc.dram_tensor("out", (BATCHES, SEQ, D), _mybir.dt.float32, kind="ExternalOutput").ap()
    build(nc, *args, out)
    r = _run(nc, [arrays], core_ids=[0])
    return r.results[0]["out"]
```

```python
from contextlib import ExitStack

import numpy as np
import concourse.bass as bass
from concourse import mybir

F32 = mybir.dt.float32
F16 = mybir.dt.float16
BF16 = mybir.dt.bfloat16
ALU = mybir.AluOpType
ACT = mybir.ActivationFunctionType
AX = mybir.AxisListType

P = 128
BATCHES, SEQ, D = 16, 256, 128
TILES = 4
BLK = TILES * P
BLOCKS = BATCHES * SEQ // BLK
NB = BLK // SEQ
QT = SEQ // P
HEADS, HD = 16, 8
HG = HEADS // 4
EXPERTS, INTER, TOPK = 160, 64, 8
ROUTED_SCALE = 2.5
GROUPS = 3
SLOTS = EXPERTS + 2
EG = SLOTS // GROUPS
PAIRS = EG // 2
CHUNKS = PAIRS * GROUPS
PAD = 16
W1KEYS = P + 2 * PAD
HF, HJ = 512, 4
EPS = 1e-5
NEG = -1e30
ROUNDS = BLOCKS // 2
N_PROJ = (2 * HG, HG + 2)
PROJ = 2 * sum(N_PROJ)
PROJ_AT = (0, N_PROJ[0], 2 * N_PROJ[0], 2 * N_PROJ[0] + N_PROJ[1])
UNITS = NB * HEADS
GRP = 4
NGRP = UNITS // GRP
HDP = 32
SEGS = (((P, 0, SEQ), (0, 0, SEQ)),
        ((0, 0, P), (P, P - 2 * PAD, P + 2 * PAD), (SEQ + 2 * PAD - P, SEQ - 2 * PAD, 2 * PAD)))
COLS = tuple(sum(n for _, _, n in segs) for segs in SEGS)
LK, LV, LC, LB, LN = 5, 7, 10, 11, 11
UNIT_SLOTS = LN + (NGRP - 1) * GRP + 1
LD, HBUF = 4, 3
OTH_FIRST, OTH_LAST = LD, CHUNKS - 2
ALONE = None
MIXED_SLOTS = (ALONE, ALONE)
NORM_SLOTS = (ALONE, ALONE, 1.0)
ROUTE_SLOTS = NORM_SLOTS + (1.0,) * 11
ATT_SLOTS = tuple(NORM_SLOTS + (2.0,) * n + (1.5,) + (1.0,) * (2 * UNIT_SLOTS) + (1.2,) * 4 for n in N_PROJ)
FFN_SLOTS = NORM_SLOTS + (2.0, ALONE, 2.0, ALONE, 2.0, ALONE, ALONE, ALONE) + (2.0,) * 2 + (1.0,) * 4
ROUTE_STEPS, ATT_STEPS, FFN_STEPS = 11, (12, 12), (4, 3)

PARAMS = {}
CONSTS = {}
for table, entries in (
    (PARAMS, (("router", EXPERTS), ("ebias", EXPERTS), ("decay", HEADS), ("qk0", 8 * P), ("qb0", 4), ("kb0", 4),
              ("v0", P), ("vb0", P), ("o0", P), ("ob0", P), ("qk1", 6 * P), ("qb1", 4), ("kb1", 2), ("v1", 16),
              ("vb1", 16), ("o1", P), ("ob1", P), ("w1", HF), ("b1", HJ), ("w2", HF), ("b2", P), ("scale", 1))),
    (CONSTS, (("ident", P), ("negdist", 4 * P), ("band", W1KEYS), ("bandT", COLS[1]), ("mq", 1), ("mk", 1), ("valid", 3),
              ("half", 2), ("selE1", 4), ("selO1", 4), ("selE2", 4), ("selO2", 4), ("diag", 4),
              ("pow", TILES)))):
    at_col = 0
    for entry, width in entries:
        table[entry] = (at_col, width)
        at_col += width
    table["_all"] = (0, at_col)


def build(nc, x, params, consts, sel16, wmoe, out):
    x_v = x.rearrange("b s d -> (b s) d").rearrange("(i t p) d -> i p t d", p=P, t=TILES)
    out_v = out.rearrange("b s d -> (b s) d").rearrange("(i t p) d -> i p t d", p=P, t=TILES)

    with ExitStack() as ctx:
        def sb(name, shape, dt=F32):
            return ctx.enter_context(nc.sbuf_tensor(name, shape, dt))

        def sem(name):
            return ctx.enter_context(nc.semaphore(name))

        par = sb("par", [P, PARAMS["_all"][1]])
        con = sb("con", [P, CONSTS["_all"][1]])
        sel = sb("sel", [2 * EG, PAIRS, P], F16)
        ident16 = sb("ident16", [P, P], F16)
        ones16 = sb("ones16", [P, P], F16)
        wm = sb("wm", [P, PAIRS, 4 * GROUPS, P], F16)
        decay16 = sb("decay16", [P, HEADS, 3 * P], BF16)
        alpha = sb("alpha", [P, 4, HEADS])
        vb1t = sb("vb1t", [P, 3, 16])
        qb0s = sb("qb0s", [P, 4])
        b2h = sb("b2h", [P, P])
        xin = sb("xin", [P, TILES, P])
        xout = sb("xout", [P, TILES, P])
        xs = [sb(f"xs{n}", [P, TILES, P]) for n in range(2)]

        xn = sb("xn", [P, TILES, P])
        xT = sb("xT", [P, NB, SEQ + 2 * PAD])
        mid = xT[:, :, PAD:PAD + SEQ]
        stats = sb("stats", [P, TILES, 6])
        mv = sb("mv", [P, TILES, 2])
        vare = sb("vare", [P, TILES])
        rstd = sb("rstd", [P, TILES])

        def xT_tile(t):
            return xT[:, t // QT, PAD + (t % QT) * P:PAD + (t % QT + 1) * P]

        mwork = sb("mwork", [P, 6, BLK])
        xh = sb("xh", [P, 2, BLK], F16)
        xl = sb("xl", [P, 2, BLK], F16)
        m8 = sb("m8", [P, TILES, TOPK])
        wsum = sb("wsum", [P, 3, TILES])
        comb16 = sb("comb16", [P, TILES, GROUPS, 2 * EG], F16)
        combT = sb("combT", [2 * EG, 2, GROUPS, BLK], F16)
        hh = sb("hh", [P, HBUF, BLK], F16)
        hl = sb("hl", [P, HBUF, BLK], F16)
        yT = xn[:].rearrange("p t d -> p (t d)")

        owork = sb("owork", [P, 4, BLK])
        probs, rep, comb = [owork[:, :, :].rearrange("p a n -> p (a n)")[:, k * TILES * EXPERTS:(k + 1) * TILES * EXPERTS]
                            .rearrange("p (t e) -> p t e", t=TILES) for k in range(3)]
        shared = sb("shared", [P, 2, BLK])
        att = shared[:, 0, :].rearrange("p (t d) -> p t d", t=TILES)
        attT = shared[:, 1, :]
        rank = shared[0:4, :, :]
        big = sb("big", [P, 4, BLK])
        pf = big[:, 0:2, :]
        oT = big[:, 2, 0:SEQ]
        weff = big[:, :, :].rearrange("p (b m) n -> p b m n", b=NB)
        hid = owork[:, :, :].rearrange("p (b r) (c q) -> p b (r c) q", b=NB, c=2)
        phi2 = sb("phi2", [P, 2, BLK], F16)
        qst = sb("qst", [P, HG, BLK], F16)
        kst0 = sb("kst0", [P, HG, NB, SEQ], F16)
        kst1 = sb("kst1", [P, 2, NB, SEQ + 2 * PAD], F16)
        va0 = sb("va0", [P, TILES, HEADS, HDP])
        va1 = sb("va1", [P, NB, 3, 2, HDP])
        nmax = sb("nmax", [P, 2, P])
        dump = big[:, 3, SEQ:].bitcast(BF16)
        nmaxT = big[:, 3, 0:SEQ].bitcast(F16).rearrange("p (k q) -> p k q", k=2)
        rden = sb("rden", [P, GRP * QT])
        odd = owork[0:4, 3, 0:2 * P]

        bank = [ctx.enter_context(nc.psum_tensor(f"bank{n}", [P, 512], F32)) for n in range(8)]
        b_gate, b_spread, b_y = bank[0:2], bank[2], bank[3]
        b_q, b_k, b_o, b_x = bank[4:8]

        def pc(name):
            a, w = PARAMS[name]
            return par[:, a:a + w]

        def cc(name, rows=P):
            a, w = CONSTS[name]
            return con[0:rows, a:a + w]

        ident = cc("ident")

        params_in, consts_in, w_in = sem("params_in"), sem("consts_in"), [sem(f"w_in{r}") for r in range(3)]
        w_hi, w_lo = sem("w_hi"), sem("w_lo")
        setup_pool, setup_dve, setup_act = sem("setup_pool"), sem("setup_dve"), sem("setup_act")
        decay_ready = sem("decay_ready")
        x_in, x_taken, out_ready, stored = sem("x_in"), sem("x_taken"), sem("out_ready"), sem("stored")
        route_step, oth_step, carried = sem("route_step"), sem("oth_step"), sem("carried")
        route_norm = [sem("route_" + name) for name in ("var_ready", "rstd_ready", "xn_ready", "xT_raw", "xT_ready")]
        oth_norm = [sem("oth_" + name) for name in ("var_ready", "rstd_ready", "xn_ready", "xT_raw", "xT_ready")]
        router_raw, logits_ready, probs_ready = sem("router_raw"), sem("logits_ready"), sem("probs_ready")
        x_split, comb_ready = sem("x_split"), sem("comb_ready")
        combT_raw, combT_ready = sem("combT_raw"), sem("combT_ready")
        gate_raw, spread_raw = sem("gate_raw"), sem("spread_raw")
        tanh_done, gated, weighted = sem("tanh_done"), sem("gated"), sem("weighted")
        h_hi, h_lo, h_used = sem("h_hi"), sem("h_lo"), sem("h_used")
        y_copied, y_tok, mixed = sem("y_copied"), sem("y_tok"), sem("mixed")
        proj_raw, proj_copied, stacked = sem("proj_raw"), sem("proj_copied"), sem("stacked")
        v_raw, v_ready = sem("v_raw"), sem("v_ready")
        scores_raw, maxed = sem("scores_raw"), sem("maxed")
        nmaxT_raw, nmaxT_ready = sem("nmaxT_raw"), sem("nmaxT_ready")
        keyside_raw, biased, exp_done = sem("keyside_raw"), sem("biased"), sem("exp_done")
        pv_done, oT_ready, turned, divided = sem("pv_done"), sem("oT_ready"), sem("turned"), sem("divided")
        attT_raw, attT_ready, out_raw = sem("attT_raw"), sem("attT_ready"), sem("out_raw")
        picked_raw, rank_ready, outer_raw, weff_ready = sem("picked_raw"), sem("rank_ready"), sem("outer_raw"), sem("weff_ready")
        hid_raw, hid_ready, down_raw = sem("hid_raw"), sem("hid_ready"), sem("down_raw")

        def at(i, q, n, per, rounds=4):
            return i * (rounds * per) + (q * per + n)

        def stage(r):
            if r < 2:
                return big[:, :, :].rearrange("p a n -> p (a n)")[:, r * 2 * GROUPS * P:(r + 1) * 2 * GROUPS * P]
            return kst0[:, :, :, :].rearrange("p g b q -> p (g b q)").bitcast(F32)[:, 0:2 * GROUPS * P]

        def piece(j, lo):
            return wm[:, j, lo:4 * GROUPS:2, :]

        assert CHUNKS % HBUF == 0 and CHUNKS % 3 == 0

        def chunk(c):
            return c // GROUPS, c % GROUPS

        def rounds(eng, route, moe, mixed_, attention, ffn):
            def interleave(mixture, stages, slots):
                shared_slots = OTH_LAST - OTH_FIRST - slots.count(ALONE)
                share = sum(w for w in slots if w is not ALONE) / shared_slots
                done, left = 0, 0.0
                for k, _ in enumerate(mixture):
                    if k < OTH_FIRST or done == len(slots):
                        continue
                    if slots[done] is ALONE:
                        next(stages)
                        done += 1
                        continue
                    left += share
                    while done < len(slots) and slots[done] is not ALONE and slots[done] <= left + 1e-6:
                        next(stages)
                        left -= slots[done]
                        done += 1
                for _ in stages:
                    pass

            def first_attention(i, n):
                def stages():
                    yield from mixed_(i, n, n)
                    yield from attention(i, n, n, 0)
                    yield from route(i, 2 + n, n, 1)
                return stages(), MIXED_SLOTS + ATT_SLOTS[0] + ROUTE_SLOTS

            def second_layer(i, n, last):
                def stages():
                    yield from mixed_(i, 2 + n, n)
                    yield from ffn(i, 2 * n, n, 0)
                    yield from attention(i, 2 + n, n, 1)
                    yield from ffn(i, 2 * n + 1, n, 1)
                    if not last:
                        yield from route(i, 4 + n, n, 0)
                return stages(), MIXED_SLOTS + FFN_SLOTS + ATT_SLOTS[1] + FFN_SLOTS + (() if last else ROUTE_SLOTS)

            def round_(i, last):
                interleave(moe(i, 1), *first_attention(i, 0))
                interleave(moe(i, 2), *first_attention(i, 1))
                interleave(moe(i, 3), *second_layer(i, 0, last))
                interleave(moe(i, 4, last), *second_layer(i, 1, last))

            for _ in route(0, 0, 0, 0):
                pass
            interleave(moe(0, 0), route(0, 1, 1, 0), ROUTE_SLOTS)
            with eng.Fori(0, ROUNDS - 1) as i:
                round_(i, False)
            round_(ROUNDS - 1, True)

        def steps_of(i, q, over):
            for c in range(LD + 1 if over else CHUNKS):
                yield q * CHUNKS + c

        def runs(i, q, n, over):
            return (q > 0 or n >= 0) and not (over and n >= q * CHUNKS)

        def count(i, n):
            return i * (4 * CHUNKS) + (n + 1)

        def oth_norm_of_attention(q):
            return (0, 1, 3, 6)[q]

        def oth_norm_of_ffn(q):
            return (2, 4, 5, 7)[q]

        block = ctx.enter_context(nc.Block())

        @block.sync
        def _(sp):
            sp.dma_start(par[:], params).then_inc(params_in, 16)
            sp.dma_start(con[:], consts).then_inc(consts_in, 16)
            sp.dma_start(xin[:], x_v[0]).then_inc(x_in, 16)
            for r in range(3):
                sp.dma_start(stage(r), wmoe[r]).then_inc(w_in[r], 16)
            sp.dma_start(sel[:], sel16[0:2 * EG, 0:PAIRS * P].rearrange("p (j m) -> p j m", m=P)).then_inc(consts_in, 16)
            sp.dma_start(ident16[:], sel16[:, PAIRS * P:]).then_inc(consts_in, 16)
            sp.wait_ge(x_taken, 1)
            sp.dma_start(xin[:], x_v[1]).then_inc(x_in, 16)
            assert PAIRS % 3 == 0
            with sp.Fori(1, PAIRS // 3) as m:
                for r in range(3):
                    sp.wait_ge(w_hi, m * 3 + (r - 2))
                    sp.wait_ge(w_lo, m * 3 + (r - 2))
                    sp.dma_start(stage(r), wmoe[m * 3 + r]).then_inc(w_in[r], 16)

            with sp.Fori(0, ROUNDS - 1) as i:
                for n in range(2):
                    sp.wait_ge(x_taken, i * 2 + (2 + n))
                    sp.dma_start(xin[:], x_v[i * 2 + (2 + n)]).then_inc(x_in, 16)
                    sp.wait_ge(out_ready, i * 2 + (1 + n))
                    sp.dma_start(out_v[i * 2 + n], xout[:]).then_inc(stored, 16)
            for n in (BLOCKS - 2, BLOCKS - 1):
                sp.wait_ge(out_ready, n + 1)
                sp.dma_start(out_v[n], xout[:]).then_inc(stored, 16)
            sp.wait_ge(stored, 16 * (BLOCKS + 1))

        @block.gpsimd
        def _(pool):
            for buffer in (xT, kst1, va0, va1, nmax, comb16):
                nc.gpsimd.memset(buffer[:], 0.0).then_inc(setup_pool, 1)
            nc.gpsimd.memset(ones16[:], 1.0).then_inc(setup_pool, 1)
            pool.wait_ge(setup_pool, 7)
            nc.gpsimd.memset(va0[:, :, :, HD:HD + 1], 1.0).then_inc(setup_pool, 1)
            nc.gpsimd.memset(va1[:, :, :, :, HD:HD + 1], 1.0).then_inc(setup_pool, 1)
            k = EXPERTS - (GROUPS - 1) * EG
            nc.gpsimd.memset(comb16[:, :, GROUPS - 1, k:k + 1], 0.5).then_inc(setup_pool, 1)
            pool.wait_ge(consts_in, 48)
            pool.wait_ge(setup_dve, 5)

            def decay_of(h):
                for to, (start, n) in ((0, (0, SEQ)), (SEQ, (3 * P, P))):
                    nc.gpsimd.tensor_scalar(decay16[:, h, to:to + n], cc("negdist")[:, start:start + n],
                                            alpha[:, 3, h:h + 1], None, ALU.mult).then_inc(decay_ready, 1)

            def root(norm, i, q, per_round):
                pool.wait_ge(norm[0], i * per_round + (q + 1))
                nc.gpsimd.tensor_tensor(rstd[:], vare[:], cc("pow"), ALU.pow).then_inc(norm[1], 1)

            def route(i, q, s, u):
                root(route_norm, i, q, 4)
                for _ in ROUTE_SLOTS:
                    yield

            def moe(i, q, over=False):
                for n in steps_of(i, q, over):
                    c = n - 3
                    if runs(i, q, c, over):
                        pool.wait_ge(h_hi, count(i, c))
                        nc.gpsimd.tensor_tensor(hl[:, c % HBUF, :], mwork[:, 3 + c % 3, :], hh[:, c % HBUF, :],
                                                ALU.subtract).then_inc(h_lo, 1)
                    if q == 0 and n % 2 == 0 and n // 2 < HEADS:
                        decay_of(n // 2)
                    yield

            def mixed_(i, q, s):
                for _ in MIXED_SLOTS:
                    yield

            def attention(i, q, s, a):
                root(oth_norm, i, oth_norm_of_attention(q), 8)
                for _ in ATT_SLOTS[a]:
                    yield

            def ffn(i, q, s, u):
                root(oth_norm, i, oth_norm_of_ffn(q), 8)
                for _ in FFN_SLOTS:
                    yield

            rounds(pool, route, moe, mixed_, attention, ffn)

        @block.tensor
        def _(pe):
            pe.wait_ge(consts_in, 48)
            pe.wait_ge(params_in, 16)
            pe.wait_ge(setup_pool, 10)

            def transposes(norm, i, q, per_round):
                pe.wait_ge(norm[2], i * per_round + (q + 1))
                for t in range(TILES):
                    mm = nc.tensor.transpose(b_x[:, t * P:(t + 1) * P], xn[:, t, :], ident)
                mm.then_inc(norm[3], 1)

            def route(i, q, s, u):
                yield
                yield
                transposes(route_norm, i, q, 4)
                yield
                pe.wait_ge(route_norm[4], at(i, q, 1, 1))
                for t in range(TILES):
                    mm = nc.tensor.matmul(bank[4 + t // 2][:, (t % 2) * 256:(t % 2) * 256 + EXPERTS],
                                          xT_tile(t), pc("router"), start=True, stop=True)
                mm.then_inc(router_raw, 1)
                for _ in range(10):
                    yield
                pe.wait_ge(comb_ready, at(i, q, 1, 1))
                for g in range(GROUPS):
                    dst = bank[6 + g // 2][:, (g % 2) * 256:(g % 2 + 1) * 256].bitcast(F16)
                    for t in range(TILES):
                        mm = nc.tensor.transpose(dst[0:2 * EG, t * P:(t + 1) * P], comb16[:, t, g, :], ident16[:, :])
                mm.then_inc(combT_raw, 1)
                yield

            def moe(i, q, over=False):
                def gate(n):
                    j, g = chunk(n % CHUNKS)
                    if q == 0:
                        pe.wait_ge(w_hi, j + 1)
                        pe.wait_ge(w_lo, j + 1)
                    if n >= 2:
                        pe.wait_ge(gated, count(i, n - 2))
                    dst = b_gate[n % 2]
                    nc.tensor.matmul(dst[:, :], wm[:, j, 4 * g, :], xh[:, q % 2, :], start=True, stop=False)
                    nc.tensor.matmul(dst[:, :], wm[:, j, 4 * g, :], xl[:, q % 2, :], start=False, stop=False)
                    nc.tensor.matmul(dst[:, :], wm[:, j, 4 * g + 1, :], xh[:, q % 2, :],
                                     start=False, stop=True).then_inc(gate_raw, 1)

                def down(n):
                    j, g = chunk(n % CHUNKS)
                    if n % CHUNKS == 0 and n > 0:
                        pe.wait_ge(y_copied, at(i, n // CHUNKS, 0, 1))
                    pe.wait_ge(h_lo, count(i, n))
                    nc.tensor.matmul(b_y[:, :], wm[:, j, 4 * g + 2, :], hh[:, n % HBUF, :],
                                     start=(n % CHUNKS == 0), stop=False)
                    nc.tensor.matmul(b_y[:, :], wm[:, j, 4 * g + 3, :], hh[:, n % HBUF, :], start=False, stop=False)
                    nc.tensor.matmul(b_y[:, :], wm[:, j, 4 * g + 2, :], hl[:, n % HBUF, :],
                                     start=False, stop=(n % CHUNKS == CHUNKS - 1)).then_inc(h_used, 1)

                def spread(n):
                    j, g = chunk(n % CHUNKS)
                    if n >= 1:
                        pe.wait_ge(weighted, count(i, n - 1))
                    nc.tensor.matmul(b_spread[:, :], sel[:, j, :], combT[:, n // CHUNKS % 2, g, :],
                                     start=True, stop=True).then_inc(spread_raw, 1)

                if not over:
                    pe.wait_ge(x_split, at(i, q, 1, 1))
                    pe.wait_ge(combT_ready, at(i, q, 1, 1))
                for n in steps_of(i, q, over):
                    if runs(i, q, n, over):
                        gate(n)
                    if runs(i, q, n - LD, over):
                        down(n - LD)
                    if runs(i, q, n - 1, over):
                        spread(n - 1)
                    yield

            def mixed_(i, q, s):
                pe.wait_ge(y_copied, at(i, q, 1, 1))
                for t in range(TILES):
                    mm = nc.tensor.transpose(b_x[:, t * P:(t + 1) * P], yT[:, t * P:(t + 1) * P], ident)
                mm.then_inc(y_tok, 1)
                yield
                yield

            def attention(i, q, s, a):
                yield
                yield
                transposes(oth_norm, i, oth_norm_of_attention(q), 8)
                yield
                wq = pc("qk0" if a == 0 else "qk1")
                pe.wait_ge(oth_norm[4], at(i, oth_norm_of_attention(q), 1, 1, 8))
                for n in range(N_PROJ[a]):
                    if n >= 3:
                        pe.wait_ge(proj_copied, i * PROJ + (PROJ_AT[q] + n - 2))
                    nc.tensor.matmul(bank[4 + n % 3][:, :], wq[:, n * P:(n + 1) * P], mid,
                                     start=True, stop=True).then_inc(proj_raw, 1)
                    yield
                if a == 0:
                    for t in range(TILES):
                        mm = nc.tensor.matmul(b_x[:, t * P:(t + 1) * P], xT_tile(t), pc("v0"), start=True, stop=True)
                else:
                    for b in range(NB):
                        for g, (key0, _, _) in enumerate(SEGS[1]):
                            c = (b * 3 + g) * 16
                            mm = nc.tensor.matmul(b_x[:, c:c + 16], xT[:, b, key0:key0 + P], pc("v1"),
                                                  start=True, stop=True)
                mm.then_inc(v_raw, 1)
                yield

                def query_side(n):
                    b, h = n // HEADS, n % HEADS
                    rows = slice(32 * (h % 4), 32 * (h % 4) + 32)
                    if n >= 1:
                        pe.wait_ge(maxed, at(i, q, n, UNITS))
                    for qt in range(QT):
                        lhs = qst[rows, h // 4, b * SEQ + qt * P:b * SEQ + (qt + 1) * P]
                        if a == 0:
                            rhs, keys = kst0[rows, h // 4, b, :], SEQ
                        else:
                            rhs, keys = kst1[rows, h // 8, b, qt * P:qt * P + W1KEYS], W1KEYS
                        mm = nc.tensor.matmul(b_q[:, qt * 256:qt * 256 + keys], lhs, rhs, start=True, stop=True)
                    mm.then_inc(scores_raw, 1)

                def turn_maxima(k):
                    pe.wait_ge(maxed, at(i, q, GRP * (k + 1), UNITS))
                    if k >= 2:
                        pe.wait_ge(divided, at(i, q, k - 1, NGRP))
                    nc.tensor.transpose(b_x[:, 0:P], nmax[:, k % 2, :], ident).then_inc(nmaxT_raw, 1)

                def key_side(n):
                    b, h = n // HEADS, n % HEADS
                    rows = slice(32 * (h % 4), 32 * (h % 4) + 32)
                    if n % GRP == 0:
                        pe.wait_ge(nmaxT_ready, at(i, q, n // GRP + 1, NGRP))
                    if n >= 1:
                        pe.wait_ge(biased, at(i, q, n, UNITS))
                    c = 0
                    for g, (key0, q0, nq) in enumerate(SEGS[a]):
                        dst = b_k[:, c:c + nq]
                        keys = kst0[rows, h // 4, b, key0:key0 + P] if a == 0 else \
                            kst1[rows, h // 8, b, key0:key0 + P]
                        nc.tensor.matmul(dst, ones16[rows, :], nmaxT[rows, n // GRP % 2, q0:q0 + nq],
                                         start=(g == 0), stop=False, skip_group_check=True)
                        mm = nc.tensor.matmul(dst, keys, qst[rows, h // 4, b * SEQ + q0:b * SEQ + q0 + nq],
                                              start=False, stop=True, skip_group_check=True)
                        c += nq
                    mm.then_inc(keyside_raw, 1)

                def values(n):
                    b, h, k = n // HEADS, n % HEADS, n // GRP
                    if n == 0:
                        pe.wait_ge(v_ready, at(i, q, 1, 1))
                    pe.wait_ge(exp_done, at(i, q, n + 1, UNITS))
                    if n % GRP == 0 and k >= 1:
                        pe.wait_ge(oT_ready, at(i, q, k, NGRP))
                    r, c = HDP * (n % GRP), 0
                    for g, (key0, q0, nq) in enumerate(SEGS[a]):
                        v = va0[:, b * QT + key0 // P, h, :] if a == 0 else va1[:, b, g, h // 8, :]
                        mm = nc.tensor.matmul(b_o[r:r + HDP, q0:q0 + nq], v, owork[:, 1 + n % 2, c:c + nq],
                                              start=(g == 0), stop=(g == len(SEGS[a]) - 1), skip_group_check=True)
                        c += nq
                    mm.then_inc(pv_done, 1)

                def turn_back(k):
                    pe.wait_ge(oT_ready, at(i, q, k + 1, NGRP))
                    pe.wait_ge(nmaxT_ready, at(i, q, min(k + 2, NGRP), NGRP))
                    if k >= 1:
                        pe.wait_ge(divided, at(i, q, k, NGRP))
                    for qt in range(QT):
                        mm = nc.tensor.transpose(b_x[:, qt * P:(qt + 1) * P], oT[:, qt * P:(qt + 1) * P], ident)
                    mm.then_inc(turned, 1)

                pe.wait_ge(stacked, i * PROJ + (PROJ_AT[q] + N_PROJ[a]))
                for slot in range(UNIT_SLOTS):
                    if slot < UNITS:
                        query_side(slot)
                    if slot % GRP == 0 and 1 <= slot // GRP <= NGRP:
                        turn_maxima(slot // GRP - 1)
                    if (slot - LB) % GRP == 0 and 0 <= (slot - LB) // GRP < NGRP:
                        turn_back((slot - LB) // GRP)
                    if 0 <= slot - LV < UNITS:
                        values(slot - LV)
                    yield
                    if 0 <= slot - LK < UNITS:
                        key_side(slot - LK)
                    yield
                pe.wait_ge(divided, at(i, q, NGRP, NGRP))
                for t in range(TILES):
                    mm = nc.tensor.transpose(b_q[:, t * P:(t + 1) * P], att[:, t, :], ident)
                mm.then_inc(attT_raw, 1)
                yield
                pe.wait_ge(attT_ready, at(i, q, 1, 1))
                for t in range(TILES):
                    mm = nc.tensor.matmul(b_k[:, t * P:(t + 1) * P], attT[:, t * P:(t + 1) * P],
                                          pc("o0" if a == 0 else "o1"), start=True, stop=True)
                mm.then_inc(out_raw, 1)
                yield
                yield
                yield

            def ffn(i, q, s, u):
                def pick(b):
                    rows = xn[:, b * QT, :]
                    nc.tensor.matmul(bank[4][0:4, 0:P], cc("selO1"), rows, start=True, stop=True)
                    nc.tensor.matmul(bank[4][0:4, P:2 * P], cc("selO2"), rows, start=True, stop=True)
                    nc.tensor.matmul(bank[5][0:4, 0:P], cc("selE1"), rows, start=True, stop=True)
                    mm = nc.tensor.matmul(bank[6][0:4, 0:P], cc("selE2"), rows, start=True, stop=True)
                    mm.then_inc(picked_raw, 1)

                def outer(b):
                    pe.wait_ge(rank_ready, at(i, q, b + 1, NB))
                    for m in range(2):
                        mm = nc.tensor.matmul(bank[4 + m][:, :], odd[:, m * P:(m + 1) * P], rank[:, m, :],
                                              start=True, stop=True)
                    mm.then_inc(outer_raw, 1)

                def hidden(b, half, dst):
                    for jj in range(2):
                        j = 2 * half + jj
                        mm = nc.tensor.matmul(dst[:, jj * SEQ:(jj + 1) * SEQ], weff[:, b, 0, j * P:(j + 1) * P],
                                              mid[:, b, :], start=True, stop=True)
                    mm.then_inc(hid_raw, 1)

                def down_tile(t):
                    for r in range(HJ):
                        mm = nc.tensor.matmul(bank[4][:, t * P:(t + 1) * P],
                                              hid[:, t // QT, r, (t % QT) * P:(t % QT + 1) * P],
                                              weff[:, t // QT, 1, r * P:(r + 1) * P],
                                              start=(r == 0), stop=(r == HJ - 1))
                    return mm

                yield
                yield
                transposes(oth_norm, i, oth_norm_of_ffn(q), 8)
                yield
                pick(0)
                yield
                yield
                outer(0)
                yield
                yield
                pe.wait_ge(weff_ready, at(i, q, 1, NB))
                pick(1)
                yield
                pe.wait_ge(oth_norm[4], at(i, oth_norm_of_ffn(q), 1, 1, 8))
                hidden(0, 0, bank[7])
                yield
                outer(1)
                yield
                pe.wait_ge(hid_ready, at(i, q, 1, 2 * NB))
                hidden(0, 1, bank[7])
                yield
                pe.wait_ge(weff_ready, at(i, q, NB, NB))
                hidden(1, 0, bank[6])
                pe.wait_ge(hid_ready, at(i, q, 2, 2 * NB))
                down_tile(0)
                yield
                hidden(1, 1, bank[7])
                down_tile(1)
                yield
                pe.wait_ge(hid_ready, at(i, q, 2 * NB, 2 * NB))
                down_tile(2)
                yield
                down_tile(3).then_inc(down_raw, 1)
                yield
                yield
                yield

            rounds(pe, route, moe, mixed_, attention, ffn)

        @block.scalar
        def _(act):
            act.wait_ge(setup_dve, 1)
            nc.scalar.activation(alpha[:, 1, :], alpha[:, 0, :], ACT.Exp, scale=-1.0).then_inc(setup_act, 1)
            act.wait_ge(setup_act, 1)
            nc.scalar.activation(alpha[:, 2, :], alpha[:, 1, :], ACT.Ln, bias=1.0).then_inc(setup_act, 1)

            def weights_high(j):
                act.wait_ge(w_in[j % 3], j // 3 * 16 + 16)
                nc.scalar.copy(piece(j, 0), stage(j % 3).rearrange("p (c n) -> p c n", n=P)).then_inc(w_hi, 1)

            weights_high(0)
            weights_high(1)

            def copy_xT(norm, i, q, per_round):
                act.wait_ge(norm[3], i * per_round + (q + 1))
                nc.scalar.copy(mid, b_x[:, :].rearrange("p (b q) -> p b q", b=NB)).then_inc(norm[4], 1)

            def route(i, q, s, u):
                yield
                yield
                copy_xT(route_norm, i, q, 4)
                yield
                yield
                act.wait_ge(logits_ready, at(i, q, 1, 1))
                nc.scalar.activation(probs, rep, ACT.Sigmoid).then_inc(probs_ready, 1)
                for _ in range(9):
                    yield
                act.wait_ge(combT_raw, at(i, q, 1, 1))
                nc.scalar.copy(combT[:, q % 2, 0:2, :],
                               bank[6][0:2 * EG, :].bitcast(F16).rearrange("p (g n) -> p g n", g=2))
                nc.scalar.copy(combT[:, q % 2, 2, :], bank[7][0:2 * EG, 0:256].bitcast(F16)).then_inc(combT_ready, 1)
                yield

            def moe(i, q, over=False):
                def high(n):
                    act.wait_ge(weighted, count(i, n))
                    if n >= HBUF:
                        act.wait_ge(h_used, count(i, n - HBUF))
                    nc.scalar.copy(hh[:, n % HBUF, :], mwork[:, 3 + n % 3, :]).then_inc(h_hi, 1)

                def tanh(n):
                    act.wait_ge(gate_raw, count(i, n))
                    if n >= 3:
                        act.wait_ge(weighted, count(i, n - 3))
                    nc.scalar.activation(mwork[:, n % 3, :], b_gate[n % 2][:, :], ACT.Tanh,
                                         scale=0.5).then_inc(tanh_done, 1)

                for n in steps_of(i, q, over):
                    if n == q * CHUNKS + LD and q > 0:
                        act.wait_ge(h_used, count(i, q * CHUNKS - 1))
                        nc.scalar.copy(yT, b_y[:, :]).then_inc(y_copied, 1)
                    if runs(i, q, n - 3, over):
                        high(n - 3)
                    if runs(i, q, n, over):
                        tanh(n)
                    if q == 0 and n % GROUPS == 0 and n // GROUPS + 2 < PAIRS:
                        weights_high(n // GROUPS + 2)
                    yield
                if q == 0:
                    act.wait_ge(w_lo, PAIRS)

            def mixed_(i, q, s):
                for _ in MIXED_SLOTS:
                    yield

            def attention(i, q, s, a):
                yield
                yield
                copy_xT(oth_norm, i, oth_norm_of_attention(q), 8)
                yield
                for n in range(N_PROJ[a]):
                    act.wait_ge(proj_raw, i * PROJ + (PROJ_AT[q] + n + 1))
                    if n >= 2:
                        act.wait_ge(stacked, i * PROJ + (PROJ_AT[q] + n - 1))
                    if n < HG:
                        bias = qb0s[:, n:n + 1] if a == 0 else pc("qb1")[:, n:n + 1]
                        scale = HD ** -0.5 if a == 0 else 1.0
                    else:
                        bias, scale = pc("kb0" if a == 0 else "kb1")[:, n - HG:n - HG + 1], 1.0
                    nc.scalar.activation(pf[:, n % 2, :], bank[4 + n % 3][:, :], ACT.Identity, bias=bias, scale=scale)
                    nc.scalar.activation(phi2[:, n % 2, :], bank[4 + n % 3][:, :], ACT.Identity,
                                         bias=bias, scale=scale).then_inc(proj_copied, 1)
                    yield
                yield

                def spread_maxima(k):
                    act.wait_ge(nmaxT_raw, at(i, q, k + 1, NGRP))
                    for qt in range(QT):
                        ins = nc.scalar.mul(nmaxT[:, k % 2, qt * P:(qt + 1) * P], b_x[:, 0:P],
                                            cc("half")[:, qt:qt + 1])
                    ins.then_inc(nmaxT_ready, 1)

                def exponent(n):
                    act.wait_ge(biased, at(i, q, n + 1, UNITS))
                    if n >= 2:
                        act.wait_ge(pv_done, at(i, q, n - 1, UNITS))
                    nc.scalar.activation(owork[:, 1 + n % 2, 0:COLS[a]], owork[:, 0, 0:COLS[a]],
                                         ACT.Exp).then_inc(exp_done, 1)

                def copy_oT(k):
                    act.wait_ge(pv_done, at(i, q, GRP * (k + 1), UNITS))
                    if k >= 1:
                        act.wait_ge(turned, at(i, q, k, NGRP))
                    nc.scalar.copy(oT, b_o[:, 0:SEQ]).then_inc(oT_ready, 1)

                for slot in range(UNIT_SLOTS):
                    yield
                    if slot % GRP == 0 and 1 <= slot // GRP <= NGRP:
                        spread_maxima(slot // GRP - 1)
                    if 0 <= slot - LK - 1 < UNITS:
                        exponent(slot - LK - 1)
                    if (slot - LC) % GRP == 0 and 0 <= (slot - LC) // GRP < NGRP:
                        copy_oT((slot - LC) // GRP)
                    yield
                act.wait_ge(attT_raw, at(i, q, 1, 1))
                nc.scalar.copy(attT, b_q[:, :]).then_inc(attT_ready, 1)
                for _ in range(4):
                    yield

            def ffn(i, q, s, u):
                def gelu(b, half, src):
                    act.wait_ge(hid_raw, at(i, q, 2 * b + half + 1, 2 * NB))
                    for jj in range(2):
                        j = 2 * half + jj
                        ins = nc.scalar.activation(hid[:, b, j, :], src[:, jj * SEQ:(jj + 1) * SEQ],
                                                   ACT.Gelu, bias=pc("b1")[:, j:j + 1])
                    ins.then_inc(hid_ready, 1)

                yield
                yield
                copy_xT(oth_norm, i, oth_norm_of_ffn(q), 8)
                for _ in range(6):
                    yield
                gelu(0, 0, bank[7])
                yield
                yield
                gelu(0, 1, bank[7])
                yield
                gelu(1, 0, bank[6])
                yield
                gelu(1, 1, bank[7])
                for _ in range(5):
                    yield

            rounds(act, route, moe, mixed_, attention, ffn)

        @block.vector
        def _(dve):
            dve.wait_ge(params_in, 16)
            dve.wait_ge(consts_in, 48)
            nc.vector.scalar_tensor_tensor(out=alpha[:, 0, :], in0=pc("decay"), scalar=-1.0, in1=pc("decay"),
                                           op0=ALU.mult, op1=ALU.max).then_inc(setup_dve, 1)
            nc.vector.tensor_scalar(qb0s[:], pc("qb0"), HD ** -0.5, None, ALU.mult).then_inc(setup_dve, 1)
            nc.vector.tensor_scalar(b2h[:], pc("b2"), 0.5, None, ALU.mult).then_inc(setup_dve, 1)
            nc.vector.tensor_tensor(vb1t[:], pc("vb1").unsqueeze(1).broadcast_to([P, 3, 16]),
                                    cc("valid").unsqueeze(2).broadcast_to([P, 3, 16]),
                                    ALU.mult).then_inc(setup_dve, 1)
            dve.wait_ge(setup_act, 2)
            nc.vector.scalar_tensor_tensor(out=alpha[:, 3, :], in0=pc("decay"), scalar=0.0, in1=alpha[:, 2, :],
                                           op0=ALU.max, op1=ALU.add).then_inc(setup_dve, 1)
            nc.vector.memset(xout[:], 0.0).then_inc(stored, 16)
            dve.wait_ge(stored, 16)
            dve.wait_ge(setup_pool, 10)
            dve.wait_ge(setup_dve, 5)

            def weights_low(j):
                dve.wait_ge(w_in[j % 3], j // 3 * 16 + 16)
                dve.wait_ge(w_hi, j + 1)
                nc.vector.tensor_tensor(piece(j, 1), stage(j % 3).rearrange("p (c n) -> p c n", n=P),
                                        piece(j, 0), ALU.subtract).then_inc(w_lo, 1)

            weights_low(0)
            weights_low(1)

            def plain_wait():
                dve.sem_inc(carried, 1)

            def steps(signal, per_round):
                place = [0, 0]

                def start(i, count):
                    place[:] = i, count

                def settle(ins, plain=False):
                    place[1] += 1
                    ins.then_inc(signal, 1)
                    dve.wait_ge(signal, place[0] * per_round + place[1])
                    if plain:
                        plain_wait()

                def counted():
                    return place[1]
                return start, settle, counted

            route_start, route_settle, route_counted = steps(route_step, 4 * ROUTE_STEPS)
            oth_start, oth_settle, oth_counted = steps(oth_step, 2 * (sum(ATT_STEPS) + sum(FFN_STEPS)))

            def layer_norm(norm, settle, x_, i, q, per_round):
                for t in range(TILES):
                    ins = nc.vector.bn_stats(stats[:, t, :], x_[:, t, :])
                settle(ins, plain=True)
                for t in range(TILES):
                    ins = nc.vector.bn_aggr(mv[:, t, :], stats[:, t, :])
                settle(ins)
                nc.vector.tensor_scalar(vare[:], mv[:, :, 1], EPS, None, ALU.add).then_inc(norm[0], 1)
                yield
                dve.wait_ge(norm[1], i * per_round + (q + 1))
                for t in range(TILES):
                    ins = nc.vector.tensor_scalar(xn[:, t, :], x_[:, t, :], mv[:, t, 0:1],
                                                  rstd[:, t:t + 1], ALU.subtract, ALU.mult)
                ins.then_inc(norm[2], 1)
                yield

            def route(i, q, s, u):
                res, settle = xs[s], route_settle
                route_start(i, q * ROUTE_STEPS)
                if u == 0:
                    n = s if q < 2 else 2 + s
                    dve.wait_ge(x_in, i * 32 + (16 * n + 16))
                    nc.vector.tensor_copy(res[:], xin[:]).then_inc(x_taken, 1)
                    dve.wait_ge(x_taken, i * 2 + (n + 1))
                yield from layer_norm(route_norm, settle, res, i, q, 4)
                yield
                yield
                dve.wait_ge(route_norm[4], at(i, q, 1, 1))
                xh_v = xh[:, q % 2, :].rearrange("p (b q) -> p b q", b=NB)
                settle(nc.vector.tensor_copy(xh_v, mid))
                dve.wait_ge(router_raw, at(i, q, 1, 1))
                for k in range(2):
                    ins = nc.vector.tensor_tensor(
                        rep[:, 2 * k:2 * k + 2, :],
                        bank[4 + k][:, :].rearrange("p (t e) -> p t e", t=2)[:, :, 0:EXPERTS],
                        pc("ebias").unsqueeze(1).broadcast_to([P, 2, EXPERTS]), ALU.add)
                ins.then_inc(logits_ready, 1)
                yield
                nc.vector.tensor_tensor(xl[:, q % 2, :].rearrange("p (b q) -> p b q", b=NB), mid, xh_v,
                                        ALU.subtract).then_inc(x_split, 1)
                yield
                dve.wait_ge(probs_ready, at(i, q, 1, 1))
                plain_wait()
                for t in range(TILES):
                    ins = nc.vector.max(m8[:, t, :], probs[:, t, :])
                settle(ins, plain=True)
                yield
                for t in range(TILES):
                    ins = nc.vector.match_replace(rep[:, t, :], m8[:, t, :], probs[:, t, :], -1.0)
                settle(nc.vector.tensor_reduce(wsum[:, 0, :], m8[:], AX.X, ALU.add))
                yield
                settle(nc.vector.tensor_scalar(wsum[:, 1, :], wsum[:, 0, :], 1e-9, None, ALU.add))
                settle(nc.vector.reciprocal(wsum[:, 2, :], wsum[:, 1, :]))
                settle(nc.vector.tensor_scalar(wsum[:, 0, :], wsum[:, 2, :], 0.5 * ROUTED_SCALE, None, ALU.mult))
                yield
                settle(nc.vector.scalar_tensor_tensor(out=rep, in0=rep, scalar=0.0, in1=probs,
                                                      op0=ALU.is_lt, op1=ALU.mult))
                yield
                settle(nc.vector.tensor_tensor(comb, rep, wsum[:, 0, :].unsqueeze(2)
                                               .broadcast_to([P, TILES, EXPERTS]), ALU.mult))
                yield
                k = EXPERTS - (GROUPS - 1) * EG
                whole = comb[:, :, 0:(GROUPS - 1) * EG].rearrange("p t (g e) -> p t g e", g=GROUPS - 1)
                part = comb[:, :, (GROUPS - 1) * EG:]
                nc.vector.tensor_copy(comb16[:, :, 0:GROUPS - 1, 0:EG], whole)
                settle(nc.vector.tensor_copy(comb16[:, :, GROUPS - 1, 0:k], part))
                yield
                nc.vector.tensor_tensor(comb16[:, :, 0:GROUPS - 1, EG:], whole, comb16[:, :, 0:GROUPS - 1, 0:EG],
                                        ALU.subtract)
                nc.vector.tensor_tensor(comb16[:, :, GROUPS - 1, EG:EG + k], part, comb16[:, :, GROUPS - 1, 0:k],
                                        ALU.subtract).then_inc(comb_ready, 1)
                dve.wait_ge(comb_ready, at(i, q, 1, 1))
                assert route_counted() == (q + 1) * ROUTE_STEPS, route_counted() - q * ROUTE_STEPS
                yield
                yield

            def moe(i, q, over=False):
                def gated_(n):
                    dve.wait_ge(tanh_done, count(i, n))
                    nc.vector.scalar_tensor_tensor(out=mwork[:, n % 3, :], in0=mwork[:, n % 3, :], scalar=1.0,
                                                   in1=b_gate[n % 2][:, :], op0=ALU.add,
                                                   op1=ALU.mult).then_inc(gated, 1)

                def weight(n):
                    if n >= 3:
                        dve.wait_ge(h_lo, count(i, n - 3))
                    dve.wait_ge(gated, count(i, n))
                    dve.wait_ge(spread_raw, count(i, n))
                    nc.vector.tensor_tensor(mwork[:, 3 + n % 3, :], mwork[:, n % 3, :], b_spread[:, :],
                                            ALU.mult).then_inc(weighted, 1)

                for n in steps_of(i, q, over):
                    if runs(i, q, n - 2, over):
                        weight(n - 2)
                    if runs(i, q, n - 1, over):
                        gated_(n - 1)
                    if q == 0 and n % GROUPS == 1 and n // GROUPS + 2 < PAIRS:
                        weights_low(n // GROUPS + 2)
                    yield
                if q == 0:
                    dve.wait_ge(w_lo, PAIRS)
                    dve.wait_ge(decay_ready, 2 * HEADS)

            def mixed_(i, q, s):
                yield
                dve.wait_ge(y_tok, at(i, q, 1, 1))
                nc.vector.scalar_tensor_tensor(out=xs[s][:], in0=tiles_of(b_x), scalar=0.5, in1=xs[s][:],
                                               op0=ALU.mult, op1=ALU.add).then_inc(mixed, 1)
                dve.wait_ge(mixed, at(i, q, 1, 1))
                yield

            def attention(i, q, s, a):
                res, settle = xs[s], oth_settle
                if q == 0:
                    oth_start(i, 0)
                before = oth_counted()
                yield from layer_norm(oth_norm, settle, res, i, oth_norm_of_attention(q), 8)
                yield
                yield
                for n in range(N_PROJ[a]):
                    phi = phi2[:, n % 2, :]
                    dve.wait_ge(proj_copied, i * PROJ + (PROJ_AT[q] + n + 1))
                    if n < HG:
                        dst, mask = qst[:, n, :].rearrange("p (b q) -> p b q", b=NB), cc("mq")
                    elif a == 0:
                        dst, mask = kst0[:, n - HG, :, :], cc("mk")
                    else:
                        dst, mask = kst1[:, n - HG, :, PAD:PAD + SEQ], cc("mk")
                    nc.vector.scalar_tensor_tensor(
                        out=dst, in0=phi.rearrange("p (b q) -> p b q", b=NB), scalar=mask,
                        in1=pf[:, n % 2, :].rearrange("p (b q) -> p b q", b=NB),
                        op0=ALU.mult, op1=ALU.add).then_inc(stacked, 1)
                    yield
                dve.wait_ge(v_raw, at(i, q, 1, 1))
                if a == 0:
                    for t in range(TILES):
                        ins = nc.vector.tensor_tensor(
                            va0[:, t, :, 0:HD], b_x[:, t * P:(t + 1) * P].rearrange("p (h d) -> p h d", d=HD),
                            pc("vb0").rearrange("p (h d) -> p h d", d=HD), ALU.add)
                else:
                    for b in range(NB):
                        ins = nc.vector.tensor_tensor(
                            va1[:, b, :, :, :].rearrange("p g k e -> p (g k) e")[:, :, 0:HD],
                            b_x[:, b * 48:(b + 1) * 48].rearrange("p (c d) -> p c d", d=HD),
                            vb1t[:].rearrange("p g (k d) -> p (g k) d", d=HD), ALU.add)
                ins.then_inc(v_ready, 1)

                def maximum(n):
                    h, k = n % HEADS, n // GRP
                    if n >= 1:
                        dve.wait_ge(maxed, at(i, q, n, UNITS))
                    dve.wait_ge(scores_raw, at(i, q, n + 1, UNITS))
                    plain_wait()
                    for qt in range(QT):
                        if a == 0:
                            keys, table = SEQ, decay16[:, h, (1 - qt) * P:(3 - qt) * P]
                        else:
                            keys, table = W1KEYS, cc("band")
                        c = 32 * (n % GRP) + qt
                        ins = nc.vector.tensor_tensor_reduce(
                            out=dump[:, qt * 256:qt * 256 + keys], in0=b_q[:, qt * 256:qt * 256 + keys], in1=table,
                            scale=-1.0, scalar=3e38, op0=ALU.add, op1=ALU.min, accum_out=nmax[:, k % 2, c:c + 1])
                    ins.then_inc(maxed, 1)

                def add_bias(n):
                    h = n % HEADS
                    if n >= 1:
                        dve.wait_ge(exp_done, at(i, q, n, UNITS))
                    dve.wait_ge(keyside_raw, at(i, q, n + 1, UNITS))
                    if a == 0:
                        ins = nc.vector.scalar_tensor_tensor(
                            out=owork[:, 0, :], in0=cc("negdist"), scalar=alpha[:, 3, h:h + 1], in1=b_k[:, :],
                            op0=ALU.mult, op1=ALU.add)
                    else:
                        ins = nc.vector.tensor_tensor(owork[:, 0, 0:COLS[1]], b_k[:, 0:COLS[1]], cc("bandT"), ALU.add)
                    ins.then_inc(biased, 1)

                def divide(k):
                    b, hg = k // HG, k % HG
                    dve.wait_ge(turned, at(i, q, k + 1, NGRP))
                    o = b_x[:, 0:SEQ].rearrange("p (c e) -> p c e", e=HDP)
                    if k >= 1:
                        dve.wait_ge(divided, at(i, q, k, NGRP))
                    settle(nc.vector.reciprocal(rden[:], o[:, :, HD]))
                    o4 = b_x[:, 0:SEQ].rearrange("p (t h e) -> p t h e", t=QT, e=HDP)[:, :, :, 0:HD]
                    r4 = rden[:].rearrange("p (t h) -> p t h", t=QT).unsqueeze(3).broadcast_to([P, QT, GRP, HD])
                    nc.vector.tensor_tensor(
                        att[:, b * QT:(b + 1) * QT, hg * GRP * HD:(hg + 1) * GRP * HD]
                        .rearrange("p t (h d) -> p t h d", d=HD), o4, r4, ALU.mult).then_inc(divided, 1)

                for slot in range(UNIT_SLOTS):
                    if 0 <= slot - LK - 1 < UNITS:
                        add_bias(slot - LK - 1)
                    yield
                    if slot < UNITS:
                        maximum(slot)
                    if (slot - LN) % GRP == 0 and 0 <= (slot - LN) // GRP < NGRP:
                        divide((slot - LN) // GRP)
                    yield
                yield
                yield
                dve.wait_ge(out_raw, at(i, q, 1, 1))
                settle(nc.vector.tensor_tensor(res[:], tiles_of(b_k), res[:], ALU.add))
                yield
                settle(nc.vector.tensor_tensor(res[:], res[:], pc("ob0" if a == 0 else "ob1").unsqueeze(1)
                                                  .broadcast_to([P, TILES, P]), ALU.add))
                assert oth_counted() == before + ATT_STEPS[a], oth_counted() - before
                yield

            def ffn(i, q, s, u):
                res, settle = xs[s], oth_settle
                before = oth_counted()

                def factors(b):
                    dve.wait_ge(picked_raw, at(i, q, b + 1, NB))
                    nc.vector.tensor_copy(odd, bank[4][0:4, 0:2 * P])
                    nc.vector.tensor_tensor(rank[:, 0, :].rearrange("p (j q) -> p j q", j=4),
                                            bank[5][0:4, 0:P].unsqueeze(1).broadcast_to([4, 4, P]),
                                            cc("diag", 4).unsqueeze(2).broadcast_to([4, 4, P]), ALU.mult)
                    ins = nc.vector.tensor_tensor(
                        rank[:, 1, :].rearrange("p (r j q) -> p r j q", r=HJ, j=4),
                        bank[6][0:4, 0:P].rearrange("p (q r) -> p r q", r=HJ).unsqueeze(2).broadcast_to([4, HJ, 4, 32]),
                        cc("diag", 4).unsqueeze(1).unsqueeze(3).broadcast_to([4, HJ, 4, 32]), ALU.mult)
                    ins.then_inc(rank_ready, 1)

                def weights(b):
                    dve.wait_ge(outer_raw, at(i, q, b + 1, NB))
                    for m, w in enumerate(("w1", "w2")):
                        ins = nc.vector.scalar_tensor_tensor(out=weff[:, b, m, :], in0=bank[4 + m][:, :],
                                                             scalar=pc("scale"), in1=pc(w),
                                                             op0=ALU.mult, op1=ALU.add)
                    ins.then_inc(weff_ready, 1)

                yield from layer_norm(oth_norm, settle, res, i, oth_norm_of_ffn(q), 8)
                yield
                yield
                for b in range(NB):
                    factors(b)
                    yield
                    yield
                    weights(b)
                    yield
                    if b == 0:
                        yield
                for _ in range(4):
                    yield
                dve.wait_ge(down_raw, at(i, q, 1, 1))
                settle(nc.vector.scalar_tensor_tensor(out=res[:], in0=tiles_of(bank[4]), scalar=0.5, in1=res[:],
                                                         op0=ALU.mult, op1=ALU.add))
                yield
                b2_v = b2h[:].unsqueeze(1).broadcast_to([P, TILES, P])
                if u == 0:
                    settle(nc.vector.tensor_tensor(res[:], res[:], b2_v, ALU.add))
                else:
                    dve.wait_ge(stored, i * 32 + (16 * s + 16))
                    nc.vector.tensor_tensor(xout[:], res[:], b2_v, ALU.add).then_inc(out_ready, 1)
                    dve.wait_ge(out_ready, i * 2 + (s + 1))
                assert oth_counted() == before + FFN_STEPS[u], oth_counted() - before
                yield

            rounds(dve, route, moe, mixed_, attention, ffn)


def tiles_of(b):
    return b[:, :].rearrange("p (t d) -> p t d", t=TILES)


def lay_out(a):
    f = np.float32

    def rows(v):
        v = np.asarray(v, f).reshape(-1)
        return np.broadcast_to(v, (P, v.size))

    heads = np.array([[(4 * g + hh) * HD + d for hh in range(4) for c in range(4) for d in range(HD)]
                      for g in range(HG)])
    kv = np.array([[k * HD + d for hh in range(4) for c in range(4) for d in range(HD)] for k in range(2)])

    def stacks(w_cols, index):
        return np.concatenate([w_cols[:, ix] for ix in index], axis=1)

    qkv_wT, qkv_b = np.asarray(a["L0_attn_qkv_w"]).T, np.asarray(a["L0_attn_qkv_b"])
    values = {
        "router": np.asarray(a["L0_ffn_router_w"]).T, "ebias": rows(a["L0_ffn_expert_bias"]),
        "decay": rows(a["L0_attn_decay_alpha"]),
        "qk0": np.concatenate([stacks(qkv_wT[:, 0:D], heads), stacks(qkv_wT[:, D:2 * D], heads)], axis=1),
        "qb0": qkv_b[0:D][heads].T, "kb0": qkv_b[D:2 * D][heads].T,
        "v0": qkv_wT[:, 2 * D:], "vb0": rows(qkv_b[2 * D:]),
        "o0": np.asarray(a["L0_attn_out_w"]).T, "ob0": rows(a["L0_attn_out_b"]),
        "qk1": np.concatenate([stacks(np.asarray(a["L1_attn_Wq"]), heads), stacks(np.asarray(a["L1_attn_Wk"]), kv)], axis=1),
        "qb1": np.asarray(a["L1_attn_bq"])[heads].T, "kb1": np.asarray(a["L1_attn_bk"])[kv].T,
        "v1": np.asarray(a["L1_attn_Wv"]), "vb1": rows(a["L1_attn_bv"]),
        "o1": np.asarray(a["L1_attn_Wo"]), "ob1": rows(a["L1_attn_bo"]),
        "w1": np.asarray(a["L1_ffn_W1"]).T, "b1": np.asarray(a["L1_ffn_b1"]).reshape(HJ, P).T,
        "w2": np.asarray(a["L1_ffn_W2"]).T.reshape(HJ, P, D).transpose(1, 0, 2).reshape(P, HJ * D),
        "b2": rows(a["L1_ffn_b2"]), "scale": rows(a["L1_ffn_scale"]),
    }
    params = np.zeros((P, PARAMS["_all"][1]), f)
    for name, v in values.items():
        at, w = PARAMS[name]
        assert v.shape == (P, w), (name, v.shape)
        params[:, at:at + w] = v

    gate = np.concatenate([np.asarray(a["L0_ffn_w_gate"]), np.asarray(a["L0_ffn_w_gate_shared"])[None],
                           np.zeros((1, INTER, D), f)])
    down = np.concatenate([np.asarray(a["L0_ffn_w_down"]), np.asarray(a["L0_ffn_w_down_shared"])[None],
                           np.zeros((1, D, INTER), f)])
    gate = gate.reshape(GROUPS, PAIRS, P, D).transpose(1, 3, 0, 2)
    down = down.transpose(0, 2, 1).reshape(GROUPS, PAIRS, P, D).transpose(1, 2, 0, 3)
    wmoe = np.ascontiguousarray(np.stack([gate, down], axis=3)).reshape(PAIRS, P, 2 * GROUPS * P)
    return params, wmoe


def shape_constants():
    f = np.float32
    p = np.arange(P)
    values = {
        "ident": np.eye(P, dtype=f),
        "negdist": np.concatenate([-np.abs(np.arange(SEQ)[None] - start - p[:, None]) for start in (P, 0)], 1).astype(f),
        "band": np.where((np.arange(W1KEYS)[None] >= p[:, None]) & (np.arange(W1KEYS)[None] < p[:, None] + 2 * PAD),
                         0.0, NEG).astype(f),
        "mq": np.where(p % 32 >= 16, -1.0, 0.0).astype(f)[:, None],
        "mk": np.where(p % 16 >= 8, -1.0, 0.0).astype(f)[:, None],
        "bandT": np.concatenate([np.where((k0 + p[:, None] >= q0 + np.arange(nq)[None])
                                          & (k0 + p[:, None] < q0 + np.arange(nq)[None] + 2 * PAD)
                                          & (k0 + p[:, None] >= floor), 0.0, NEG)
                                 for (k0, q0, nq), floor in zip(SEGS[1], (0, P, SEQ))], 1).astype(f),
        "valid": np.stack([(k0 + p >= PAD) & (k0 + p < PAD + SEQ) for k0, _, _ in SEGS[1]], 1).astype(f),
        "half": (p[:, None] % QT == np.arange(QT)[None]).astype(f),
        "pow": np.full((P, TILES), -0.5, f),
        "diag": (p[:, None] == np.arange(4)[None]).astype(f),
    }
    for name, first in (("selE1", 1), ("selO1", 2), ("selE2", 9), ("selO2", 10)):
        values[name] = (p[:, None] == first + 2 * np.arange(4)[None]).astype(f)
    consts = np.zeros((P, CONSTS["_all"][1]), f)
    for name, v in values.items():
        at, w = CONSTS[name]
        assert v.shape == (P, w), (name, v.shape)
        consts[:, at:at + w] = v
    sel16 = np.zeros((P, (PAIRS + 1) * P), np.float16)
    for j in range(PAIRS):
        for m in range(P):
            sel16[2 * j + m // INTER, j * P + m] = 1
            sel16[EG + 2 * j + m // INTER, j * P + m] = 1
    sel16[:, PAIRS * P:(PAIRS + 1) * P] = np.eye(P)
    return consts, sel16


def kernel(**inputs):
    import numpy as _np
    import concourse.bacc as _bacc
    from concourse import mybir as _mybir
    from concourse.bass_utils import run_bass_kernel_spmd as _run

    params, wmoe = lay_out(inputs)
    consts, sel16 = shape_constants()
    nc = _bacc.Bacc("TRN2", target_bir_lowering=False, num_devices=1)
    arrays = {"x": _np.ascontiguousarray(inputs["L0_attn_x"]), "params": params, "consts": consts,
              "sel16": sel16, "wmoe": wmoe}
    args = [nc.dram_tensor(name, v.shape, _mybir.dt.from_np(v.dtype), kind="ExternalInput").ap()
            for name, v in arrays.items()]
    out = nc.dram_tensor("out", (BATCHES, SEQ, D), _mybir.dt.float32, kind="ExternalOutput").ap()
    build(nc, *args, out)
    r = _run(nc, [arrays], core_ids=[0])
    return r.results[0]["out"]
```
